# Optimizing a Trainium2 kernel written in Bass

```python
import numpy as np
import jax
import jax.numpy as jnp

def _softmax(x, axis=-1):
    return jax.nn.softmax(x, axis=axis)

def _gelu(x):
    return jax.nn.gelu(x, approximate=True)

def _silu(x):
    return jax.nn.silu(x)

def _sigmoid(x):
    return jax.nn.sigmoid(x)

def _layernorm(x, axis=-1, eps=1e-05):
    m = jnp.mean(x, axis=axis, keepdims=True)
    v = jnp.var(x, axis=axis, keepdims=True)
    return (x - m) / jnp.sqrt(v + eps)

def _scatter_add(tgt, idx, src, axis=0):
    return tgt.at[idx].add(src)

def _segment_sum(src, seg, n):
    return jax.ops.segment_sum(src, seg, n)
kernel_name = 'mk_xattn_seq_d1_seqx_r8_3158ad'

def setup_inputs(seed: int=0):
    np.random.seed(seed)
    _w = jnp.asarray

    def _rec_inputs():
        import jax
        import jax.numpy as jnp
        _rk = jax.random.key(seed)
        x = -0.000719 + 1.001 * jax.random.normal(jax.random.fold_in(_rk, 1), (16, 128, 160), jnp.float32)
        _lenS = 128 - jax.random.randint(jax.random.fold_in(_rk, 7), (16,), 0, max(1, 128 // 4) + 1, jnp.int32)
        _lenS2 = 128 - jax.random.randint(jax.random.fold_in(_rk, 8), (16,), 0, max(1, 128 // 4) + 1, jnp.int32)
        _ctx_2048P = jax.random.normal(jax.random.fold_in(_rk, 11), (16, 16, 256), jnp.float32)
        _ctx_2048c = jax.random.dirichlet(jax.random.fold_in(_rk, 511), 0.3 * jnp.ones((16,), jnp.float32), (16, 128))
        _ctx_2048t = jnp.einsum('bsk,bkd->bsd', _ctx_2048c, _ctx_2048P)
        _ctx_2048t = _ctx_2048t * jax.lax.rsqrt(jnp.mean(jnp.square(_ctx_2048t)) + 1e-12) * 0.953939
        ctx_2048 = 0.00257118 + 0.99863 * (_ctx_2048t + 0.3 * jax.random.normal(jax.random.fold_in(_rk, 611), (16, 128, 256), jnp.float32))
        fside_S_0 = jax.random.uniform(jax.random.fold_in(_rk, 12), (128,), jnp.float32, 0.0, 0.999706)
        return (x, ctx_2048, fside_S_0)
    x, ctx_2048, fside_S_0 = _rec_inputs()

    def _L0_xattn_setup():
        import jax, jax.numpy as jnp
        import numpy as np
        HEADS = 20
        NUM_TOKENS = 4
        IP_SCALE = 1.0
        SEM_SCALE = 0.5
        RESCALE = 1.0
        EPS = 1e-12

        def _l2norm(x, axis=-1):
            n = jnp.sqrt(jnp.sum(x * x, axis=axis, keepdims=True))
            return x / jnp.maximum(n, EPS)
        key = jax.random.key(seed)
        ks = jax.random.split(key, 10)
        B, S, C = (2, 128, 160)
        T, E = (81, 256)
        inp = {'hidden_states': jax.random.normal(ks[0], (B, S, C), jnp.float32), 'encoder_hidden_states': jax.random.normal(ks[1], (B, T, E), jnp.float32), 'spatial_mask': jax.random.uniform(ks[2], (S,), jnp.float32), 'W_q': jax.random.normal(ks[3], (C, C), jnp.float32) * C ** (-0.5), 'W_k': jax.random.normal(ks[4], (E, C), jnp.float32) * E ** (-0.5), 'W_v': jax.random.normal(ks[5], (E, C), jnp.float32) * E ** (-0.5), 'W_k_ip': jax.random.normal(ks[6], (E, C), jnp.float32) * E ** (-0.5), 'W_v_ip': jax.random.normal(ks[7], (E, C), jnp.float32) * E ** (-0.5), 'W_out': jax.random.normal(ks[8], (C, C), jnp.float32) * C ** (-0.5), 'b_out': jnp.zeros((C,), jnp.float32)}
        return inp
    _L0_xattn_all = _L0_xattn_setup()
    _L0_xattn_in = {k: v for k, v in _L0_xattn_all.items() if k in ('W_q', 'W_k', 'W_v', 'W_k_ip', 'W_v_ip', 'W_out', 'b_out')}
    del _L0_xattn_all
    return {'x': x, 'ctx_2048': ctx_2048, 'fside_S_0': fside_S_0, 'L0_xattn_W_q': _L0_xattn_in['W_q'], 'L0_xattn_W_k': _L0_xattn_in['W_k'], 'L0_xattn_W_v': _L0_xattn_in['W_v'], 'L0_xattn_W_k_ip': _L0_xattn_in['W_k_ip'], 'L0_xattn_W_v_ip': _L0_xattn_in['W_v_ip'], 'L0_xattn_W_out': _L0_xattn_in['W_out'], 'L0_xattn_b_out': _L0_xattn_in['b_out']}

def reference(x, ctx_2048, fside_S_0, L0_xattn_W_q, L0_xattn_W_k, L0_xattn_W_v, L0_xattn_W_k_ip, L0_xattn_W_v_ip, L0_xattn_W_out, L0_xattn_b_out):
    import jax
    import jax.numpy as jnp

    def _L0_xattn_ref(hidden_states, encoder_hidden_states, spatial_mask, W_q, W_k, W_v, W_k_ip, W_v_ip, W_out, b_out):
        import jax, jax.numpy as jnp
        import numpy as np
        HEADS = 20
        NUM_TOKENS = 4
        IP_SCALE = 1.0
        SEM_SCALE = 0.5
        RESCALE = 1.0
        EPS = 1e-12

        def _l2norm(x, axis=-1):
            n = jnp.sqrt(jnp.sum(x * x, axis=axis, keepdims=True))
            return x / jnp.maximum(n, EPS)
        B, S, C = hidden_states.shape
        H = HEADS
        Dh = C // H
        attn_scale = Dh ** (-0.5)
        residual = hidden_states
        text_ehs = encoder_hidden_states[:, :-NUM_TOKENS]
        ip_ehs = encoder_hidden_states[:, -NUM_TOKENS:]

        def heads(x):
            return x.reshape(B, -1, H, Dh).transpose(0, 2, 1, 3)
        q = heads(hidden_states @ W_q)
        k_t = heads(text_ehs @ W_k)
        v_t = heads(text_ehs @ W_v)
        scores_t = jnp.einsum('bhsd,bhtd->bhst', q, k_t) * attn_scale
        probs_t = jax.nn.softmax(scores_t, axis=-1)
        text_out = jnp.einsum('bhst,bhtd->bhsd', probs_t, v_t)
        text_out = text_out.transpose(0, 2, 1, 3).reshape(B, S, C)
        k_ip = heads(ip_ehs @ W_k_ip)
        v_ip = heads(ip_ehs @ W_v_ip)
        attn_scores = jnp.einsum('bhsd,bhnd->bhsn', q, k_ip) * attn_scale
        qsem = jnp.einsum('bhst,bte->bhse', probs_t, text_ehs)
        qsem = _l2norm(qsem)
        ip_n = _l2norm(ip_ehs)
        sem = jnp.einsum('bhse,bne->bhsn', qsem, ip_n)
        sem = jax.lax.stop_gradient(sem)
        fused = attn_scores + SEM_SCALE * sem
        probs_ip = jax.nn.softmax(fused, axis=-1)
        probs_ip = probs_ip * spatial_mask[None, None, :, None]
        ip_out = jnp.einsum('bhsn,bhnd->bhsd', probs_ip, v_ip)
        ip_out = ip_out.transpose(0, 2, 1, 3).reshape(B, S, C)
        out = text_out + IP_SCALE * ip_out
        out = out @ W_out + b_out
        out = out + residual
        return out / RESCALE
    x = _L0_xattn_ref(x, ctx_2048, fside_S_0, L0_xattn_W_q, L0_xattn_W_k, L0_xattn_W_v, L0_xattn_W_k_ip, L0_xattn_W_v_ip, L0_xattn_W_out, L0_xattn_b_out)
    return x

_drawn_inputs = setup_inputs


def setup_inputs(seed=0):
    import zlib

    import numpy as np

    out = dict(_drawn_inputs(seed))
    spreads = {'L0_xattn_b_out': (0.0, 0.1)}
    factors = {}
    for name, (base, spread) in spreads.items():
        noise = np.random.default_rng([zlib.crc32(name.encode()), seed]).standard_normal(out[name].shape)
        drawn = base * np.exp(spread * noise) if base else spread * noise
        out[name] = jnp.asarray(drawn.astype(out[name].dtype))
    for name, factor in factors.items():
        out[name] = (out[name] * factor).astype(out[name].dtype)
    return out
```

```python
from contextlib import ExitStack

import concourse.bass as bass
from concourse import mybir

F32 = mybir.dt.float32
F32R = mybir.dt.float32r
ALU = mybir.AluOpType
ACT = mybir.ActivationFunctionType
AX_X = mybir.AxisListType.X

B, S, C = 16, 128, 160
H, D = 20, 8
T, NIP, E = 124, 4, 256
TOK = T + NIP
EC = E // 128
CH = C // 2
CP = 96
HG = 4
G = H // HG
PG = HG // 2
NPAIR = H // 2
SCALE = float(D) ** -0.5
EPS2 = 1e-24
MAIN = D + 1 + NIP + T
RW = MAIN + NIP + 1 + D - 0 - NIP + NIP
SMALL = 2 * (D + 1 + NIP)
BANK = 512


def xattn_program(nc, xT, xn, ctxT, ipT, ipn, smask, wq, wkv, wkvip, wout, ident, ipmask, kip_d, vip_d, out):
    assert RW == 2 * (D + 1 + NIP) + T
    with ExitStack() as ctx:
        def sb(name, shape, dt=F32):
            return ctx.enter_context(nc.sbuf_tensor(name, shape, dt))

        def sem(name):
            return ctx.enter_context(nc.semaphore(name))

        def two(make, name, *a):
            return [make(f"{name}{p}", *a) for p in range(2)]

        wq_sb = sb("wq_sb", [CP, 2, C])
        wq_scaled = sb("wq_scaled", [CP, 2, C])
        wkv_sb = sb("wkv_sb", [128, EC, 2 * C])
        wkvip_sb = sb("wkvip_sb", [128, EC, 2 * C])
        wout_sb = sb("wout_sb", [CP, 2, C])
        ident_sb = sb("ident_sb", [128, 128])
        ipmask_sb = sb("ipmask_sb", [NIP * H, C])
        smask_sb = sb("smask_sb", [S, 1])
        ipT_sb = sb("ipT_sb", [128, EC, B * NIP])
        ip_sb = sb("ip_sb", [B * NIP, E])
        ip_junk = sb("ip_junk", [B * NIP, E])
        ip_ss = sb("ip_ss", [B * NIP, 3])
        ipunit = sb("ipunit", [B * NIP, E])
        ipunitT = sb("ipunitT", [128, EC, B * NIP])
        kip_split = sb("kip_split", [B * NIP, H, 2, 2, D])
        vip_sb = sb("vip_sb", [B * NIP, C])
        xT_sb = two(sb, "xT_sb", [CP, 2, S])
        xn_sb = two(sb, "xn_sb", [S, C])
        ctxT_sb = two(sb, "ctxT_sb", [128, EC, TOK])
        g_stage = sb("g_stage", [T, NIP + TOK])
        v_stage = sb("v_stage", [T, C])
        k_split = sb("k_split", [TOK, H, 2, 2, D])
        q_split = sb("q_split", [S, H, 2, 2, D])
        k_stack = sb("k_stack", [128, G, TOK])
        q_stack = two(sb, "q_stack", [128, G, S], F32R)
        k_diag = two(sb, "k_diag", [128, G, HG, TOK], F32R)
        main_rhs = two(sb, "main_rhs", [T, NPAIR, RW])
        negmax = two(sb, "negmax", [S, H])
        probs = two(sb, "probs", [S, H, T])
        probsT = two(sb, "probsT", [T, HG, S])
        norm2 = two(sb, "norm2", [S, H])
        small = two(sb, "small", [S, NPAIR, SMALL])
        ip_score = two(sb, "ip_score", [S, H, NIP])
        junk = sb("junk", [S, 2 * PG, T])
        one = sb("one", [128, 1])
        exponent = sb("exponent", [S, H])
        guard = sb("guard", [S, H])
        clamped = sb("clamped", [S, H])
        rnorm = sb("rnorm", [S, H])
        rden = sb("rden", [S, H])
        fused = sb("fused", [S, H, NIP])
        centred = sb("centred", [S, H, NIP])
        half = sb("half", [S, H, 2])
        ipmax = sb("ipmax", [S, H])
        ip_exp = sb("ip_exp", [S, H, NIP])
        ipsum = sb("ipsum", [S, H])
        rip = sb("rip", [S, H])
        rip_masked = sb("rip_masked", [S, H])
        ip_probs = sb("ip_probs", [S, H, NIP])
        text = sb("text", [S, C])
        vrep = two(sb, "vrep", [NIP * H, C])
        v_diag = two(sb, "v_diag", [CP, C])
        ip_probsT = sb("ip_probsT", [CP, S])
        oT = sb("oT", [CP, 2, S])
        out_sb = two(sb, "out_sb", [S, C])

        def bank(name):
            return ctx.enter_context(nc.psum_tensor(name, [128, BANK], F32))

        score_ps = two(bank, "score_ps")
        probsT_ps = two(bank, "probsT_ps")
        main_ps = two(bank, "main_ps")
        pa = bank("pa")
        pb = bank("pb")

        s_const = sem("s_const")
        s_ipin = sem("s_ipin")
        s_kip_out = sem("s_kip_out")
        s_vip_out = sem("s_vip_out")
        s_ctx_in = two(sem, "s_ctx_in")
        s_xT_in = two(sem, "s_xT_in")
        s_xn_in = two(sem, "s_xn_in")
        s_vrep_in = two(sem, "s_vrep_in")
        s_kip_in = sem("s_kip_in")
        s_grep = two(sem, "s_grep")
        s_kd03 = two(sem, "s_kd03")
        s_kd4 = two(sem, "s_kd4")
        s_store = two(sem, "s_store")
        s_init = sem("s_init")
        s_ipv = sem("s_ipv")
        s_iprn = sem("s_iprn")
        s_ipp = sem("s_ipp")
        s_ctx_mm = sem("s_ctx_mm")
        s_q_mm = sem("s_q_mm")
        s_kT = sem("s_kT")
        s_kq4 = sem("s_kq4")
        s_qT = sem("s_qT")
        s_scores = sem("s_scores")
        s_transp = sem("s_transp")
        s_main = sem("s_main")
        s_pipT_mm = sem("s_pipT_mm")
        s_outT_mm = sem("s_outT_mm")
        s_final_mm = sem("s_final_mm")
        s_gstage = sem("s_gstage")
        s_khi = sem("s_khi")
        s_qhi = sem("s_qhi")
        s_kst03 = sem("s_kst03")
        s_st4 = sem("s_st4")
        s_qst03 = sem("s_qst03")
        s_exp = sem("s_exp")
        s_probsT = sem("s_probsT")
        s_ipexp = sem("s_ipexp")
        s_klo = sem("s_klo")
        s_qlo = sem("s_qlo")
        s_max = sem("s_max")
        s_norm = sem("s_norm")
        s_stats = sem("s_stats")
        s_ipmax = sem("s_ipmax")
        s_rip = sem("s_rip")
        s_pipT = sem("s_pipT")
        s_oT = sem("s_oT")
        s_final = sem("s_final")
        s_ipcol = sem("s_ipcol")
        s_vcopy = sem("s_vcopy")
        s_rnorm = sem("s_rnorm")
        s_fuse = sem("s_fuse")
        s_ipsum = sem("s_ipsum")
        s_ipprobs = sem("s_ipprobs")
        s_text = sem("s_text")
        s_vdiag = sem("s_vdiag")

        block = ctx.enter_context(nc.Block())

        def doubled(cols):
            r = cols.rearrange("t (h d) -> t h d", d=D)
            return r.unsqueeze(2).broadcast_to([r.shape[0], H, 2, D])

        def windows(eng, window):
            for w in (-1, 0, 1):
                window(w, w % 2, w // 2, w)
            with eng.Fori(1, B // 2 - 1) as i:
                for p in range(2):
                    window(i * 2 + p, p, i, None)
            for w in (B - 2, B - 1, B, B + 1):
                window(w, w % 2, w // 2, w)

        def has(w, lag=0, ahead=0):
            return w is None or 0 <= w - lag + ahead < B

        def has_group(w, g, lag):
            return w is None or 0 <= G * w + g - lag < G * B

        def wait(eng, s, value):
            if isinstance(value, int) and value <= 0:
                return
            eng.wait_ge(s, value)

        @block.sync
        def _(sp):
            sp.dma_start(ipT_sb[:, :, :], ipT).then_inc(s_ipin, 16)
            sp.dma_start(ip_sb[:, :], ipn).then_inc(s_ipin, 16)
            sp.dma_start(wkvip_sb[:, :, :], wkvip).then_inc(s_ipin, 16)
            sp.dma_start(ident_sb[:, :], ident).then_inc(s_ipin, 16)
            sp.wait_ge(s_init, 1)
            sp.dma_start(wkv_sb[:, :, :], wkv).then_inc(s_const, 16)
            for b in range(2):
                sp.dma_start(ctxT_sb[b][:, :, 0:T], ctxT[b]).then_inc(s_ctx_in[b], 16)
                sp.dma_start(xT_sb[b][0:CH, :, :], xT[b]).then_inc(s_xT_in[b], 16)
                if b == 0:
                    sp.dma_start(wq_sb[0:CH, :, :], wq).then_inc(s_const, 16)
            sp.dma_start(smask_sb[:, :], smask).then_inc(s_const, 16)
            sp.dma_start(ipmask_sb[:, :], ipmask).then_inc(s_const, 16)
            sp.dma_start(wout_sb[0:CH + 1, :, :], wout).then_inc(s_const, 16)
            sp.wait_ge(s_ipv, 2)
            sp.dma_start(kip_d, kip_split[:, :, :, :, :].rearrange("t h c a d -> t (h c a d)")).then_inc(s_kip_out, 16)
            sp.wait_ge(s_ipv, 3)
            sp.dma_start(vip_d, vip_sb[:, :]).then_inc(s_vip_out, 16)
            sp.wait_ge(s_kip_out, 16)
            sp.wait_ge(s_vip_out, 16)

            def window(b, p, i, w):
                n = 1 - p
                if has(w, ahead=1):
                    wait(sp, s_kT, b + 1)
                    wait(sp, s_kq4, b + 1)
                    sp.dma_start(k_split[T:TOK, :, :, :, :].rearrange("t h c a d -> t (h c a d)"),
                                 kip_d[bass.ds((b + 1) * NIP, NIP), :]).then_inc(s_kip_in, 16)
                if has(w) and has(w, ahead=2):
                    wait(sp, s_ctx_mm, b + 1)
                    sp.dma_start(ctxT_sb[p][:, :, 0:T], ctxT[b + 2]).then_inc(s_ctx_in[p], 16)
                    wait(sp, s_q_mm, b + 1)
                    sp.dma_start(xT_sb[p][0:CH, :, :], xT[b + 2]).then_inc(s_xT_in[p], 16)
                if has(w, ahead=1):
                    wait(sp, s_main, NPAIR * b)
                    wait(sp, s_gstage, b + 2)
                    sp.dma_start(main_rhs[n][:, :, D + 1:D + 1 + NIP + TOK],
                                 g_stage[:, :].unsqueeze(1).broadcast_to([T, NPAIR, NIP + TOK])).then_inc(s_grep[n], 16)
                    wait(sp, s_scores, G * b)
                    wait(sp, s_kst03, b + 2)
                    for j in range(HG):
                        sp.dma_start(k_diag[n][32 * j:32 * j + 32, 0:G - 1, j, :].bitcast(F32),
                                     k_stack[32 * j:32 * j + 32, 0:G - 1, :]).then_inc(s_kd03[n], 16)
                if has(w):
                    wait(sp, s_vdiag, b - 1)
                    sp.dma_start(vrep[p][:, :], bass.AP(vip_d.tensor, vip_d.offset + b * (NIP * C),
                                                        [[0, H], [C, NIP], [1, C]])).then_inc(s_vrep_in[p], 16)
                if has(w, ahead=1):
                    wait(sp, s_st4, b + 2)
                    for j in range(HG):
                        sp.dma_start(k_diag[n][32 * j:32 * j + 32, G - 1, j, :].bitcast(F32),
                                     k_stack[32 * j:32 * j + 32, G - 1, :]).then_inc(s_kd4[n], 16)
                if has(w, lag=2):
                    wait(sp, s_final, b - 1)
                    sp.dma_start(out[b - 2], out_sb[p][:, :]).then_inc(s_store[p], 16)
                if has(w):
                    wait(sp, s_final, b - 1)
                    sp.dma_start(xn_sb[p][:, :], xn[b]).then_inc(s_xn_in[p], 16)

            windows(sp, window)
            for p in range(2):
                sp.wait_ge(s_store[p], 16 * (B // 2))

        @block.gpsimd
        def _(pool):
            pool.memset(xT_sb[0][:, :, :], 0.0)
            pool.memset(xT_sb[1][:, :, :], 0.0)
            pool.memset(wq_sb[:, :, :], 0.0)
            pool.memset(wout_sb[:, :, :], 0.0).then_inc(s_init, 1)
            pool.memset(main_rhs[0][:, :, :], 1.0)
            pool.memset(main_rhs[1][:, :, :], 1.0)
            pool.memset(v_diag[0][:, :], 0.0)
            pool.memset(v_diag[1][:, :], 0.0)
            pool.memset(ip_probsT[:, :], 0.0)
            pool.memset(oT[:, :, :], 1.0).then_inc(s_init, 1)
            pool.memset(one[:, :], 1.0)
            pool.memset(exponent[:, :], -0.5).then_inc(s_init, 1)
            pool.wait_ge(s_ipv, 5)
            pool.wait_ge(s_init, 3)
            pool.tensor_tensor(ip_ss[:, 2:3], ip_ss[:, 1:2], exponent[0:B * NIP, 0:1], ALU.pow).then_inc(s_iprn, 1)
            pool.wait_ge(s_ipv, 8)
            for b in range(2):
                pool.tensor_copy(ctxT_sb[b][:, :, T:TOK], ipunitT[:, :, b * NIP:(b + 1) * NIP]).then_inc(s_ipcol, 1)
            pool.wait_ge(s_init, 2)
            pool.wait_ge(s_const, 16 * 5)
            pool.tensor_scalar(wq_scaled[:, :, :], wq_sb[:, :, :], SCALE, None, ALU.mult).then_inc(s_init, 1)

            def window(b, p, i, w):
                n = 1 - p
                if has(w) and has(w, ahead=2):
                    wait(pool, s_ctx_mm, b + 1)
                    pool.tensor_copy(ctxT_sb[p][:, :, T:TOK],
                                     ipunitT[:, :, bass.ds((b + 2) * NIP, NIP)]).then_inc(s_ipcol, 1)
                if has(w, ahead=1):
                    wait(pool, s_khi, b + 2)
                    wait(pool, s_main, NPAIR * b)
                    r = main_rhs[n]
                    vs = v_stage[:, :].rearrange("t (r a d) -> t r a d", a=2, d=D)
                    ones = one[0:T, 0:1].unsqueeze(2).broadcast_to([T, NPAIR, D])
                    pool.tensor_tensor(r[:, :, 0:D], vs[:, :, 0, :], ones, ALU.mult)
                    pool.tensor_tensor(r[:, :, RW - D:RW], vs[:, :, 1, :], ones, ALU.mult).then_inc(s_vcopy, 1)
                if has(w):
                    wait(pool, s_vrep_in[p], 16 * (i + 1))
                    wait(pool, s_outT_mm, b - 1)
                    pool.tensor_tensor(v_diag[p][0:NIP * H, :], vrep[p][:, :], ipmask_sb[:, :],
                                       ALU.mult).then_inc(s_vdiag, 1)
                if has(w, lag=1):
                    sm = small[n]
                    num = bass.AP(sm, 0, [[NPAIR * SMALL, S], [SMALL, NPAIR], [SMALL - NIP, 2], [1, NIP]])
                    den = bass.AP(sm, NIP + 1, [[NPAIR * SMALL, S], [SMALL, NPAIR], [D, 2], [1, D]])
                    wait(pool, s_stats, 3 * b)
                    pool.tensor_tensor(rnorm[:, :], clamped[:, :], exponent[:, :], ALU.pow).then_inc(s_rnorm, 1)
                    wait(pool, s_rnorm, b)
                    pool.tensor_tensor(fused[:, :, :].rearrange("s (r a) m -> s r a m", a=2), num,
                                       rnorm[:, :].rearrange("s (r a) -> s r a", a=2).unsqueeze(3)
                                       .broadcast_to([S, NPAIR, 2, NIP]), ALU.mult).then_inc(s_fuse, 1)
                    wait(pool, s_fuse, 3 * (b - 1) + 1)
                    pool.tensor_tensor(fused[:, :, :], fused[:, :, :], ip_score[n][:, :, :], ALU.add).then_inc(s_fuse, 1)
                    wait(pool, s_ipmax, b)
                    pool.tensor_tensor(centred[:, :, :], fused[:, :, :],
                                       ipmax[:, :].unsqueeze(2).broadcast_to([S, H, NIP]), ALU.subtract).then_inc(s_fuse, 1)
                    wait(pool, s_outT_mm, b - 1)
                    pool.tensor_tensor(text[:, :].rearrange("s (r a d) -> s r a d", a=2, d=D), den,
                                       rden[:, :].rearrange("s (r a) -> s r a", a=2).unsqueeze(3)
                                       .broadcast_to([S, NPAIR, 2, D]), ALU.mult).then_inc(s_text, 1)
                    wait(pool, s_ipexp, b)
                    pool.tensor_tensor(half[:, :, :], ip_exp[:, :, 0:2], ip_exp[:, :, 2:4], ALU.add).then_inc(s_ipsum, 1)
                    wait(pool, s_ipsum, 2 * (b - 1) + 1)
                    pool.tensor_tensor(ipsum[:, :], half[:, :, 0], half[:, :, 1], ALU.add).then_inc(s_ipsum, 1)
                    wait(pool, s_rip, b)
                    pool.tensor_tensor(rip_masked[:, :], rip[:, :], smask_sb[:, 0:1].broadcast_to([S, H]),
                                       ALU.mult).then_inc(s_ipprobs, 1)
                    wait(pool, s_ipprobs, 2 * (b - 1) + 1)
                    wait(pool, s_pipT_mm, b - 1)
                    pool.tensor_tensor(ip_probs[:, :, :], ip_exp[:, :, :],
                                       rip_masked[:, :].unsqueeze(2).broadcast_to([S, H, NIP]), ALU.mult).then_inc(s_ipprobs, 1)

            windows(pool, window)

        @block.scalar
        def _(act):
            def window(b, p, i, w):
                n = 1 - p
                for g in range(G):
                    grp = b * G + g
                    if has_group(w, g, 1):
                        t = grp - 1
                        tp = (p * G + g - 1) % 2
                        wait(act, s_transp, t + 1)
                        wait(act, s_main, PG * t - PG)
                        act.activation(probsT[tp][:, :, :].rearrange("t h s -> t (h s)"), probsT_ps[tp][0:T, :],
                                       ACT.Copy).then_inc(s_probsT, 1)
                    if has(w):
                        act.wait_ge(s_max, grp + 1)
                        for j in range(HG):
                            h = HG * g + j
                            last = act.activation(probs[p][:, h, :], score_ps[(p * G + g) % 2][:, j * TOK:j * TOK + T],
                                                  ACT.Exp, bias=negmax[p][:, h:h + 1])
                        last.then_inc(s_exp, 1)
                    if g == 0 and has(w, ahead=1):
                        wait(act, s_ctx_mm, b + 2)
                        wait(act, s_grep[p], 16 * (i + 1) if w is None or w >= 0 else 0)
                        act.activation(g_stage[:, NIP:NIP + TOK], pa[0:T, 0:TOK], ACT.Copy)
                        act.activation(g_stage[:, 0:NIP], pa[0:T, T:TOK], ACT.Copy).then_inc(s_gstage, 1)
                        wait(act, s_vcopy, b + 1)
                        act.activation(v_stage[:, :], pa[0:T, TOK:TOK + C], ACT.Copy)
                        act.activation(k_split[0:T, :, :, 0, :].bitcast(F32R), doubled(pa[0:T, TOK + C:TOK + 2 * C]),
                                       ACT.Copy).then_inc(s_khi, 1)
                    if g == 2 and has(w, ahead=1):
                        wait(act, s_q_mm, b + 2)
                        act.activation(q_split[:, :, 0, :, :].bitcast(F32R), doubled(pb[:, 0:C]),
                                       ACT.Copy).then_inc(s_qhi, 1)
                        wait(act, s_kT, b + 2)
                        if w is None or w >= 0:
                            act.wait_ge(s_kd03[p], 64 * (i + 1))
                            act.wait_ge(s_kd4[p], 64 * (i + 1))
                        act.activation(k_stack[:, 0:G - 1, :].rearrange("r g t -> r (g t)"), pa[:, :],
                                       ACT.Copy).then_inc(s_kst03, 1)
                    if g == 3 and has(w, ahead=1):
                        wait(act, s_kq4, b + 2)
                        act.activation(k_stack[:, G - 1, :], pb[:, 0:TOK], ACT.Copy)
                        act.activation(q_stack[n][:, G - 1, :], pb[:, TOK:TOK + S], ACT.Copy).then_inc(s_st4, 1)
                        wait(act, s_qT, b + 2)
                        act.activation(q_stack[n][:, 0:G - 1, :].rearrange("r g t -> r (g t)"), pa[:, :],
                                       ACT.Copy).then_inc(s_qst03, 1)
                    if g == 3 and has(w, lag=1):
                        act.wait_ge(s_fuse, 3 * b)
                        wait(act, s_ipprobs, 2 * (b - 1))
                        act.activation(ip_exp[:, :, :], centred[:, :, :], ACT.Exp).then_inc(s_ipexp, 1)

            windows(act, window)

        @block.vector
        def _(dve):
            for p in range(2):
                last = dve.memset(k_diag[p][:, :, :, :].bitcast(F32), 0.0)
            last.then_inc(s_ipv, 1)
            dve.wait_ge(s_ipp, 1)
            kips = doubled(pa[0:B * NIP, 0:C])
            dve.tensor_copy(kip_split[:, :, :, 0, :].bitcast(F32R), kips).then_inc(s_klo, 1)
            dve.wait_ge(s_klo, 1)
            dve.tensor_tensor(kip_split[:, :, :, 1, :].bitcast(F32R), kips, kip_split[:, :, :, 0, :],
                              ALU.subtract).then_inc(s_ipv, 1)
            dve.tensor_copy(vip_sb[:, :], pa[0:B * NIP, C:2 * C]).then_inc(s_ipv, 1)
            dve.wait_ge(s_ipin, 16 * 4)
            dve.tensor_tensor_reduce(ip_junk[:, :], ip_sb[:, :], ip_sb[:, :], 1.0, 0.0, ALU.mult, ALU.add,
                                     ip_ss[:, 0:1]).then_inc(s_ipv, 1)
            dve.wait_ge(s_ipv, 4)
            dve.tensor_scalar(ip_ss[:, 1:2], ip_ss[:, 0:1], EPS2, None, ALU.max).then_inc(s_ipv, 1)
            dve.wait_ge(s_iprn, 1)
            dve.tensor_scalar(ipunit[:, :], ip_sb[:, :], ip_ss[:, 2:3], 0.5, ALU.mult, ALU.mult).then_inc(s_ipv, 1)
            dve.wait_ge(s_ipp, 2)
            dve.tensor_copy(ipunitT[:, :, :].rearrange("p c t -> p (c t)"), pb[:, 0:EC * B * NIP]).then_inc(s_ipv, 2)
            dve.wait_ge(s_init, 2)

            def window(b, p, i, w):
                n = 1 - p
                for g in range(G):
                    grp = b * G + g
                    if has(w):
                        dve.wait_ge(s_scores, grp + 1)
                        if g == 0:
                            wait(dve, s_fuse, 3 * (b - 1))
                        sc = score_ps[(p * G + g) % 2][:, :].rearrange("s (h t) -> s h t", t=TOK)
                        dve.tensor_copy(ip_score[p][:, HG * g:HG * g + HG, :], sc[:, :, T:TOK])
                        dve.tensor_reduce(negmax[p][:, HG * g:HG * g + HG], sc[:, :, 0:T], AX_X, ALU.max,
                                          negate=True).then_inc(s_max, 1)
                    if g == 1 and has(w, ahead=1):
                        wait(dve, s_khi, b + 2)
                        dve.tensor_tensor(k_split[0:T, :, :, 1, :].bitcast(F32R), doubled(pa[0:T, TOK + C:TOK + 2 * C]),
                                          k_split[0:T, :, :, 0, :], ALU.subtract).then_inc(s_klo, 1)
                    if g == 3 and has(w, ahead=1):
                        wait(dve, s_qhi, b + 2)
                        dve.tensor_tensor(q_split[:, :, 1, :, :].bitcast(F32R), doubled(pb[:, 0:C]),
                                          q_split[:, :, 0, :, :], ALU.subtract).then_inc(s_qlo, 1)
                    if g == 3 and has(w, lag=1):
                        dve.wait_ge(s_fuse, 3 * (b - 1) + 2)
                        dve.tensor_reduce(ipmax[:, :], fused[:, :, :], AX_X, ALU.max).then_inc(s_ipmax, 1)
                    if has_group(w, g, 3):
                        wb = p if g >= 3 else n
                        gg = (g - 3) % G
                        if gg == 0:
                            wait(dve, s_text, b - 1 if g >= 3 else b - 2)
                        for r in range(PG):
                            pair = grp * PG + r - 3 * PG
                            wait(dve, s_norm, pair - 1)
                            dve.wait_ge(s_main, pair + 1)
                            for a in range(2):
                                h = HG * gg + 2 * r + a
                                u = main_ps[r][:, a * (T + SMALL):a * (T + SMALL) + T]
                                dve.tensor_tensor_reduce(junk[:, 2 * r + a, :], u, probs[wb][:, h, :], 1.0, 0.0, ALU.mult, ALU.add,
                                                         norm2[wb][:, h:h + 1])
                            dve.tensor_copy(small[wb][:, PG * gg + r, :],
                                            main_ps[r][:, T:T + SMALL]).then_inc(s_norm, 1)
                    if g == 2 and has(w, lag=1):
                        den = bass.AP(small[n], NIP, [[NPAIR * SMALL, S], [SMALL, NPAIR], [2 * D + 1, 2]])
                        dve.wait_ge(s_norm, NPAIR * b)
                        g3 = guard[:, :].rearrange("s (r a) -> s r a", a=2)
                        wait(dve, s_text, b - 1)
                        dve.scalar_tensor_tensor(out=g3, in0=den, scalar=EPS2, in1=den, op0=ALU.mult,
                                                 op1=ALU.mult).then_inc(s_stats, 1)
                        dve.reciprocal(rden[:, :].rearrange("s (r a) -> s r a", a=2), den).then_inc(s_stats, 1)
                        dve.wait_ge(s_stats, 3 * (b - 1) + 1)
                        dve.tensor_tensor(clamped[:, :], norm2[n][:, :], guard[:, :], ALU.max).then_inc(s_stats, 1)
                    if g == 4 and has(w, lag=1):
                        dve.wait_ge(s_ipsum, 2 * b)
                        wait(dve, s_ipprobs, 2 * (b - 1))
                        dve.reciprocal(rip[:, :], ipsum[:, :]).then_inc(s_rip, 1)
                    if g == 0 and has(w, lag=2):
                        dve.wait_ge(s_pipT_mm, b - 1)
                        dve.tensor_copy(ip_probsT[0:NIP * H, :], pb[0:NIP * H, 0:S]).then_inc(s_pipT, 1)
                    if g == 1 and has(w, lag=2):
                        dve.wait_ge(s_outT_mm, b - 1)
                        dve.tensor_copy(oT[0:CH, :, :].rearrange("c a s -> c (a s)"), pb[0:CH, 0:2 * S]).then_inc(s_oT, 1)
                    if g == 4 and has(w, lag=2):
                        dve.wait_ge(s_final_mm, b - 1)
                        dve.wait_ge(s_xn_in[p], 16 * i)
                        wait(dve, s_store[p], 16 * (i - 1))
                        dve.tensor_tensor(out_sb[p][:, :], pb[:, 0:C], xn_sb[p][:, :], ALU.add).then_inc(s_final, 1)

            windows(dve, window)

        @block.tensor
        def _(pe):
            pe.wait_ge(s_ipin, 16 * 4)
            for c in range(EC):
                mm = pe.matmul(pa[0:B * NIP, 0:2 * C], ipT_sb[:, c, :], wkvip_sb[:, c, :], start=(c == 0), stop=(c == EC - 1))
            mm.then_inc(s_ipp, 1)
            pe.wait_ge(s_ipv, 6)
            for c in range(EC):
                mm = pe.transpose(pb[:, c * B * NIP:(c + 1) * B * NIP], ipunit[:, c * 128:(c + 1) * 128],
                                  ident_sb[0:B * NIP, 0:B * NIP])
            mm.then_inc(s_ipp, 1)
            pe.wait_ge(s_ipv, 8)
            pe.wait_ge(s_const, 16 * 5)
            pe.wait_ge(s_init, 4)

            def stacked(split, g):
                return split[:, HG * g:HG * g + HG, :, :, :].rearrange("t h a b d -> t (h a b d)")

            def window(b, p, i, w):
                n = 1 - p
                i_next = i + p
                for g in range(G):
                    grp = b * G + g
                    if has(w):
                        if g == 0:
                            wait(pe, s_kd03[p], 64 * (i + 1))
                            wait(pe, s_qst03, b + 1)
                        if g == G - 1:
                            wait(pe, s_kd4[p], 64 * (i + 1))
                        wait(pe, s_exp, grp - 1)
                        pe.matmul(score_ps[(p * G + g) % 2][:, :], q_stack[p][:, g, :],
                                  k_diag[p][:, g, :, :].rearrange("r h t -> r (h t)"), start=True,
                                  stop=True).then_inc(s_scores, 1)
                    if has_group(w, g, 1):
                        tg, tb = (g - 1) % G, (p if g >= 1 else n)
                        tp = (p * G + g - 1) % 2
                        pe.wait_ge(s_exp, grp)
                        wait(pe, s_probsT, grp - 2)
                        for j in range(HG):
                            mm = pe.transpose(probsT_ps[tp][0:T, j * S:(j + 1) * S], probs[tb][:, HG * tg + j, :],
                                              ident_sb[:, :])
                        mm.then_inc(s_transp, 1)

                    if g == 0 and has(w, ahead=1):
                        wait(pe, s_ctx_in[n], 16 * (i_next + 1))
                        wait(pe, s_ipcol, b + 2)
                        wait(pe, s_qst03, b + 1)
                        for lo, width, rhs in ((0, TOK, None), (TOK, C, 0), (TOK + C, C, C)):
                            for c in range(EC):
                                r = ctxT_sb[n][:, c, :] if rhs is None else wkv_sb[:, c, rhs:rhs + C]
                                mm = pe.matmul(pa[:, lo:lo + width], ctxT_sb[n][:, c, :], r, start=(c == 0), stop=(c == EC - 1))
                        mm.then_inc(s_ctx_mm, 1)
                    if g == 0 and has(w, lag=2):
                        pe.wait_ge(s_ipprobs, 2 * (b - 1))
                        wait(pe, s_final, b - 2)
                        wait(pe, s_st4, b + 1 if has(w) else 0)
                        pe.transpose(pb[0:NIP * H, 0:S], ip_probs[:, :, :].rearrange("s h m -> s (h m)"),
                                     ident_sb[:, :]).then_inc(s_pipT_mm, 1)
                    if g == 1 and has(w, lag=2):
                        pe.wait_ge(s_pipT, b - 1)
                        pe.wait_ge(s_text, b - 1)
                        pe.wait_ge(s_vdiag, b - 1)
                        for c in range(2):
                            pe.matmul(pb[0:CH, c * S:(c + 1) * S], text[:, c * CH:(c + 1) * CH], ident_sb[:, :],
                                      start=True, stop=False)
                            mm = pe.matmul(pb[0:CH, c * S:(c + 1) * S], v_diag[p][:, c * CH:(c + 1) * CH], ip_probsT[:, :],
                                           start=False, stop=True)
                        mm.then_inc(s_outT_mm, 1)
                    if g == 2 and has(w, ahead=1):
                        wait(pe, s_xT_in[n], 16 * (i_next + 1))
                        wait(pe, s_oT, b - 1)
                        wait(pe, s_st4, b + 1)
                        for c in range(2):
                            mm = pe.matmul(pb[:, 0:C], xT_sb[n][:, c, :], wq_scaled[:, c, :], start=(c == 0), stop=(c == 1))
                        mm.then_inc(s_q_mm, 1)
                        wait(pe, s_klo, b + 3)
                        wait(pe, s_kip_in, 16 * (b + 2))
                        for k in range(G - 1):
                            mm = pe.transpose(pa[:, k * TOK:(k + 1) * TOK], stacked(k_split, k), ident_sb[:, :])
                        mm.then_inc(s_kT, 1)
                    if g == 3 and has(w, ahead=1):
                        wait(pe, s_qlo, b + 2)
                        pe.transpose(pb[:, 0:TOK], stacked(k_split, G - 1), ident_sb[:, :])
                        pe.transpose(pb[:, TOK:TOK + S], stacked(q_split, G - 1), ident_sb[:, :]).then_inc(s_kq4, 1)
                        wait(pe, s_kst03, b + 2)
                        for k in range(G - 1):
                            mm = pe.transpose(pa[:, k * S:(k + 1) * S], stacked(q_split, k), ident_sb[:, :])
                        mm.then_inc(s_qT, 1)
                    if g == 4 and has(w, lag=2):
                        pe.wait_ge(s_oT, b - 1)
                        if has(w, ahead=1):
                            wait(pe, s_st4, b + 2)
                        for c in range(2):
                            mm = pe.matmul(pb[:, 0:C], oT[:, c, :], wout_sb[:, c, :], start=(c == 0), stop=(c == 1))
                        mm.then_inc(s_final_mm, 1)

                    if has_group(w, g, 2):
                        mg, mb = (g - 2) % G, (p if g >= 2 else n)
                        mp = (p * G + g - 2) % 2
                        if mg == 0:
                            wait(pe, s_grep[mb], 16 * (i + 1))
                            wait(pe, s_vcopy, b + 1)
                        pe.wait_ge(s_probsT, grp - 1)
                        for r in range(PG):
                            pair = grp * PG + r - 2 * PG
                            wait(pe, s_norm, pair - 1)
                            blk = main_rhs[mb][:, PG * mg + r, :]
                            pe.matmul(main_ps[r][:, 0:MAIN], probsT[mp][:, 2 * r, :], blk[:, RW - MAIN:RW],
                                      start=True, stop=True)
                            pe.matmul(main_ps[r][:, MAIN:2 * MAIN], probsT[mp][:, 2 * r + 1, :], blk[:, 0:MAIN],
                                      start=True, stop=True).then_inc(s_main, 1)

            windows(pe, window)


def kernel(x, ctx_2048, fside_S_0, L0_xattn_W_q, L0_xattn_W_k, L0_xattn_W_v, L0_xattn_W_k_ip, L0_xattn_W_v_ip,
           L0_xattn_W_out, L0_xattn_b_out):
    import numpy as np
    import concourse.bacc as bacc
    from concourse.bass_utils import run_bass_kernel_spmd

    def chunks(a, n):
        return np.ascontiguousarray(np.moveaxis(a.reshape(n, a.shape[0] // n, *a.shape[1:]), 0, 1))

    x = np.asarray(x)
    cx = np.asarray(ctx_2048)
    wk, wv, wkip, wvip = (np.asarray(a) for a in (L0_xattn_W_k, L0_xattn_W_v, L0_xattn_W_k_ip, L0_xattn_W_v_ip))
    wv_swapped = wv.reshape(E, NPAIR, 2, D)[:, :, ::-1].reshape(E, C)
    wout = np.asarray(L0_xattn_W_out)
    wout_rows = np.zeros((CH + 1, 2, C), np.float32)
    wout_rows[:CH] = chunks(wout, 2)
    wout_rows[CH, 1] = np.asarray(L0_xattn_b_out)
    ip = np.ascontiguousarray(cx[:, T:].reshape(B * NIP, E))
    ipmask = np.zeros((H, NIP, H, D), np.float32)
    for h in range(H):
        ipmask[h, :, h] = 1.0
    arrays = {
        "xT": np.ascontiguousarray(x.reshape(B, S, 2, CH).transpose(0, 3, 2, 1)),
        "xn": np.ascontiguousarray(x),
        "ctxT": np.ascontiguousarray(cx[:, :T].reshape(B, T, EC, 128).transpose(0, 3, 2, 1)),
        "ipT": np.ascontiguousarray(ip.reshape(B * NIP, EC, 128).transpose(2, 1, 0)),
        "ipn": ip,
        "smask": np.ascontiguousarray(np.asarray(fside_S_0).reshape(S, 1)),
        "wq": chunks(np.asarray(L0_xattn_W_q), 2),
        "wkv": chunks(np.concatenate([wv_swapped, wk], 1), EC),
        "wkvip": chunks(np.concatenate([wkip, wvip], 1), EC),
        "wout": wout_rows,
        "ident": np.eye(128, dtype=np.float32),
        "ipmask": ipmask.reshape(H * NIP, C),
    }
    nc = bacc.Bacc("TRN2", target_bir_lowering=False, num_devices=1)
    args = {name: nc.dram_tensor(name, a.shape, mybir.dt.from_np(a.dtype), kind="ExternalInput").ap()
            for name, a in arrays.items()}
    kip_d = nc.dram_tensor("kip_d", (B * NIP, 4 * C), F32, kind="Internal").ap()
    vip_d = nc.dram_tensor("vip_d", (B * NIP, C), F32, kind="Internal").ap()
    out = nc.dram_tensor("out", (B, S, C), F32, kind="ExternalOutput").ap()
    xattn_program(nc, **args, kip_d=kip_d, vip_d=vip_d, out=out)
    r = run_bass_kernel_spmd(nc, [arrays], core_ids=[0])
    return r.results[0]["out"]
```

```python
from contextlib import ExitStack

import concourse.bass as bass
from concourse import mybir

F32 = mybir.dt.float32
F32R = mybir.dt.float32r
ALU = mybir.AluOpType
ACT = mybir.ActivationFunctionType
AX_X = mybir.AxisListType.X

B, S, C = 16, 128, 160
H, D = 20, 8
T, NIP, E = 124, 4, 256
TOK = T + NIP
EC = E // 128
CH = C // 2
CP = 96
HG = 4
G = H // HG
PG = HG // 2
NPAIR = H // 2
SCALE = float(D) ** -0.5
EPS2 = 1e-24
MAIN = D + 1 + NIP + T
RW = MAIN + NIP + 1 + D - 0 - NIP + NIP
SMALL = 2 * (D + 1 + NIP)
BANK = 512


def xattn_program(nc, xT, xn, ctxT, ipT, ipn, smask, wq, wkv, wkvip, wout, ident, ipmask, kip_d, vip_d, out):
    assert RW == 2 * (D + 1 + NIP) + T
    with ExitStack() as ctx:
        def sb(name, shape, dt=F32):
            return ctx.enter_context(nc.sbuf_tensor(name, shape, dt))

        def sem(name):
            return ctx.enter_context(nc.semaphore(name))

        def two(make, name, *a):
            return [make(f"{name}{p}", *a) for p in range(2)]

        wq_sb = sb("wq_sb", [CP, 2, C])
        wq_scaled = sb("wq_scaled", [CP, 2, C])
        wkv_sb = sb("wkv_sb", [128, EC, 2 * C])
        wkvip_sb = sb("wkvip_sb", [128, EC, 2 * C])
        wout_sb = sb("wout_sb", [CP, 2, C])
        ident_sb = sb("ident_sb", [128, 128])
        ipmask_sb = sb("ipmask_sb", [NIP * H, C])
        smask_sb = sb("smask_sb", [S, 1])
        ipT_sb = sb("ipT_sb", [128, EC, B * NIP])
        ip_sb = sb("ip_sb", [B * NIP, E])
        ip_junk = sb("ip_junk", [B * NIP, E])
        ip_ss = sb("ip_ss", [B * NIP, 3])
        ipunit = sb("ipunit", [B * NIP, E])
        ipunitT = sb("ipunitT", [128, EC, B * NIP])
        kip_split = sb("kip_split", [B * NIP, H, 2, 2, D])
        vip_sb = sb("vip_sb", [B * NIP, C])
        xT_sb = two(sb, "xT_sb", [CP, 2, S])
        xn_sb = two(sb, "xn_sb", [S, C])
        ctxT_sb = two(sb, "ctxT_sb", [128, EC, TOK])
        g_stage = sb("g_stage", [T, NIP + TOK])
        v_stage = sb("v_stage", [T, C])
        k_split = sb("k_split", [TOK, H, 2, 2, D])
        q_split = sb("q_split", [S, H, 2, 2, D])
        k_stack = sb("k_stack", [128, G, TOK])
        q_stack = two(sb, "q_stack", [128, G, S], F32R)
        k_diag = two(sb, "k_diag", [128, G, HG, TOK], F32R)
        main_rhs = two(sb, "main_rhs", [T, NPAIR, RW])
        negmax = two(sb, "negmax", [S, H])
        probs = two(sb, "probs", [S, H, T])
        probsT = two(sb, "probsT", [T, HG, S])
        norm2 = two(sb, "norm2", [S, H])
        small = two(sb, "small", [S, NPAIR, SMALL])
        ip_score = two(sb, "ip_score", [S, H, NIP])
        junk = sb("junk", [S, 2 * PG, T])
        one = sb("one", [128, 1])
        exponent = sb("exponent", [S, H])
        guard = sb("guard", [S, H])
        clamped = sb("clamped", [S, H])
        rnorm = sb("rnorm", [S, H])
        rden = sb("rden", [S, H])
        ip_stage = sb("ip_stage", [S, H, NIP])
        fused = sb("fused", [S, H, NIP])
        centred = sb("centred", [S, H, NIP])
        half = sb("half", [S, H, 2])
        ipmax = sb("ipmax", [S, H])
        ip_exp = sb("ip_exp", [S, H, NIP])
        ipsum = sb("ipsum", [S, H])
        rip = sb("rip", [S, H])
        rip_masked = sb("rip_masked", [S, H])
        ip_probs = sb("ip_probs", [S, H, NIP])
        text = sb("text", [S, C])
        vrep = two(sb, "vrep", [NIP * H, C])
        v_diag = two(sb, "v_diag", [CP, C])
        ip_probsT = sb("ip_probsT", [CP, S])
        oT = sb("oT", [CP, 2, S])
        out_sb = two(sb, "out_sb", [S, C])

        def bank(name):
            return ctx.enter_context(nc.psum_tensor(name, [128, BANK], F32))

        score_ps = two(bank, "score_ps")
        probsT_ps = two(bank, "probsT_ps")
        main_ps = two(bank, "main_ps")
        pa = bank("pa")
        pb = bank("pb")

        s_const = sem("s_const")
        s_ipin = sem("s_ipin")
        s_kip_out = sem("s_kip_out")
        s_vip_out = sem("s_vip_out")
        s_ctx_in = two(sem, "s_ctx_in")
        s_xT_in = two(sem, "s_xT_in")
        s_xn_in = two(sem, "s_xn_in")
        s_vrep_in = two(sem, "s_vrep_in")
        s_kip_in = sem("s_kip_in")
        s_grep = two(sem, "s_grep")
        s_kd03 = two(sem, "s_kd03")
        s_kd4 = two(sem, "s_kd4")
        s_store = two(sem, "s_store")
        s_init = sem("s_init")
        s_ipv = sem("s_ipv")
        s_iprn = sem("s_iprn")
        s_ipp = sem("s_ipp")
        s_ctx_mm = sem("s_ctx_mm")
        s_q_mm = sem("s_q_mm")
        s_kT = sem("s_kT")
        s_kq4 = sem("s_kq4")
        s_qT = sem("s_qT")
        s_scores = sem("s_scores")
        s_transp = sem("s_transp")
        s_main = sem("s_main")
        s_pipT_mm = sem("s_pipT_mm")
        s_outT_mm = sem("s_outT_mm")
        s_final_mm = sem("s_final_mm")
        s_gstage = sem("s_gstage")
        s_khi = sem("s_khi")
        s_qhi = sem("s_qhi")
        s_kst03 = sem("s_kst03")
        s_st4 = sem("s_st4")
        s_qst03 = sem("s_qst03")
        s_exp = sem("s_exp")
        s_probsT = sem("s_probsT")
        s_ipexp = sem("s_ipexp")
        s_klo = sem("s_klo")
        s_qlo = sem("s_qlo")
        s_max = sem("s_max")
        s_norm = sem("s_norm")
        s_stats = sem("s_stats")
        s_ipmax = sem("s_ipmax")
        s_rip = sem("s_rip")
        s_pipT = sem("s_pipT")
        s_oT = sem("s_oT")
        s_final = sem("s_final")
        s_ipcol = sem("s_ipcol")
        s_vcopy = sem("s_vcopy")
        s_rnorm = sem("s_rnorm")
        s_ipstage = sem("s_ipstage")
        s_fuse = sem("s_fuse")
        s_ipsum = sem("s_ipsum")
        s_ipprobs = sem("s_ipprobs")
        s_text = sem("s_text")
        s_vdiag = sem("s_vdiag")

        block = ctx.enter_context(nc.Block())

        def doubled(cols):
            r = cols.rearrange("t (h d) -> t h d", d=D)
            return r.unsqueeze(2).broadcast_to([r.shape[0], H, 2, D])

        def windows(eng, window):
            for w in range(-1, 4):
                window(w, w % 2, w // 2, w)
            with eng.Fori(2, B // 2 - 1) as i:
                for p in range(2):
                    window(i * 2 + p, p, i, None)
            for w in range(B - 2, B + 3):
                window(w, w % 2, w // 2, w)

        def has(w, lag=0, ahead=0):
            return w is None or 0 <= w - lag + ahead < B

        def has_group(w, g, lag):
            return w is None or 0 <= G * w + g - lag < G * B

        def wait(eng, s, value):
            if isinstance(value, int) and value <= 0:
                return
            eng.wait_ge(s, value)

        @block.sync
        def _(sp):
            sp.dma_start(ipT_sb[:, :, :], ipT).then_inc(s_ipin, 16)
            sp.dma_start(ip_sb[:, :], ipn).then_inc(s_ipin, 16)
            sp.dma_start(wkvip_sb[:, :, :], wkvip).then_inc(s_ipin, 16)
            sp.dma_start(ident_sb[:, :], ident).then_inc(s_ipin, 16)
            sp.wait_ge(s_init, 1)
            sp.dma_start(wkv_sb[:, :, :], wkv).then_inc(s_const, 16)
            for b in range(2):
                sp.dma_start(ctxT_sb[b][:, :, 0:T], ctxT[b]).then_inc(s_ctx_in[b], 16)
                sp.dma_start(xT_sb[b][0:CH, :, :], xT[b]).then_inc(s_xT_in[b], 16)
                if b == 0:
                    sp.dma_start(wq_sb[0:CH, :, :], wq).then_inc(s_const, 16)
            sp.dma_start(smask_sb[:, :], smask).then_inc(s_const, 16)
            sp.dma_start(ipmask_sb[:, :], ipmask).then_inc(s_const, 16)
            sp.dma_start(wout_sb[0:CH + 1, :, :], wout).then_inc(s_const, 16)
            sp.wait_ge(s_ipv, 2)
            sp.dma_start(kip_d, kip_split[:, :, :, :, :].rearrange("t h c a d -> t (h c a d)")).then_inc(s_kip_out, 16)
            sp.wait_ge(s_ipv, 3)
            sp.dma_start(vip_d, vip_sb[:, :]).then_inc(s_vip_out, 16)
            sp.wait_ge(s_kip_out, 16)
            sp.wait_ge(s_vip_out, 16)

            def window(b, p, i, w):
                n = 1 - p
                if has(w, ahead=1):
                    wait(sp, s_kT, b + 1)
                    wait(sp, s_kq4, b + 1)
                    sp.dma_start(k_split[T:TOK, :, :, :, :].rearrange("t h c a d -> t (h c a d)"),
                                 kip_d[bass.ds((b + 1) * NIP, NIP), :]).then_inc(s_kip_in, 16)
                if has(w) and has(w, ahead=2):
                    wait(sp, s_ctx_mm, b + 1)
                    sp.dma_start(ctxT_sb[p][:, :, 0:T], ctxT[b + 2]).then_inc(s_ctx_in[p], 16)
                    wait(sp, s_q_mm, b + 1)
                    sp.dma_start(xT_sb[p][0:CH, :, :], xT[b + 2]).then_inc(s_xT_in[p], 16)
                if has(w, lag=2):
                    wait(sp, s_final, b - 3)
                    sp.dma_start(xn_sb[p][:, :], xn[b - 2]).then_inc(s_xn_in[p], 16)
                    wait(sp, s_vdiag, b - 3)
                    sp.dma_start(vrep[p][:, :], bass.AP(vip_d.tensor, vip_d.offset + (b - 2) * (NIP * C),
                                                        [[0, H], [C, NIP], [1, C]])).then_inc(s_vrep_in[p], 16)
                if has(w, ahead=1):
                    wait(sp, s_scores, G * b)
                    wait(sp, s_kst03, b + 2)
                    for j in range(HG):
                        sp.dma_start(k_diag[n][32 * j:32 * j + 32, 0:G - 1, j, :].bitcast(F32),
                                     k_stack[32 * j:32 * j + 32, 0:G - 1, :]).then_inc(s_kd03[n], 16)
                    wait(sp, s_main, NPAIR * b)
                    wait(sp, s_gstage, b + 2)
                    sp.dma_start(main_rhs[n][:, :, D + 1:D + 1 + NIP + TOK],
                                 g_stage[:, :].unsqueeze(1).broadcast_to([T, NPAIR, NIP + TOK])).then_inc(s_grep[n], 16)
                    wait(sp, s_st4, b + 2)
                    for j in range(HG):
                        sp.dma_start(k_diag[n][32 * j:32 * j + 32, G - 1, j, :].bitcast(F32),
                                     k_stack[32 * j:32 * j + 32, G - 1, :]).then_inc(s_kd4[n], 16)
                if has(w, lag=3):
                    wait(sp, s_final, b - 2)
                    sp.dma_start(out[b - 3], out_sb[n][:, :]).then_inc(s_store[n], 16)

            windows(sp, window)
            for p in range(2):
                sp.wait_ge(s_store[p], 16 * (B // 2))

        @block.gpsimd
        def _(pool):
            pool.memset(xT_sb[0][:, :, :], 0.0)
            pool.memset(xT_sb[1][:, :, :], 0.0)
            pool.memset(wq_sb[:, :, :], 0.0)
            pool.memset(wout_sb[:, :, :], 0.0).then_inc(s_init, 1)
            pool.memset(main_rhs[0][:, :, :], 1.0)
            pool.memset(main_rhs[1][:, :, :], 1.0)
            pool.memset(v_diag[0][:, :], 0.0)
            pool.memset(v_diag[1][:, :], 0.0)
            pool.memset(ip_probsT[:, :], 0.0)
            pool.memset(oT[:, :, :], 1.0).then_inc(s_init, 1)
            pool.memset(one[:, :], 1.0)
            pool.memset(exponent[:, :], -0.5).then_inc(s_init, 1)
            pool.wait_ge(s_ipv, 5)
            pool.wait_ge(s_init, 3)
            pool.tensor_tensor(ip_ss[:, 2:3], ip_ss[:, 1:2], exponent[0:B * NIP, 0:1], ALU.pow).then_inc(s_iprn, 1)
            pool.wait_ge(s_ipv, 8)
            for b in range(2):
                pool.tensor_copy(ctxT_sb[b][:, :, T:TOK], ipunitT[:, :, b * NIP:(b + 1) * NIP]).then_inc(s_ipcol, 1)
            pool.wait_ge(s_init, 2)
            pool.wait_ge(s_const, 16 * 5)
            pool.tensor_scalar(wq_scaled[:, :, :], wq_sb[:, :, :], SCALE, None, ALU.mult).then_inc(s_init, 1)

            def per_head(t, width):
                return t[:, :].rearrange("s (r a) -> s r a", a=2).unsqueeze(3).broadcast_to([S, NPAIR, 2, width])

            def window(b, p, i, w):
                n = 1 - p
                if has(w, lag=2):
                    num = bass.AP(small[p], 0, [[NPAIR * SMALL, S], [SMALL, NPAIR], [SMALL - NIP, 2], [1, NIP]])
                    v_sum = bass.AP(small[p], NIP + 1, [[NPAIR * SMALL, S], [SMALL, NPAIR], [D, 2], [1, D]])
                    wait(pool, s_rnorm, b - 1)
                    pool.tensor_tensor(fused[:, :, :].rearrange("s (r a) m -> s r a m", a=2), num,
                                       per_head(rnorm, NIP), ALU.mult).then_inc(s_fuse, 1)
                    wait(pool, s_fuse, 3 * (b - 2) + 1)
                    wait(pool, s_ipstage, b - 1)
                    pool.tensor_tensor(fused[:, :, :], fused[:, :, :], ip_stage[:, :, :], ALU.add).then_inc(s_fuse, 1)
                    wait(pool, s_outT_mm, b - 2)
                    pool.tensor_tensor(text[:, :].rearrange("s (r a d) -> s r a d", a=2, d=D), v_sum,
                                       per_head(rden, D), ALU.mult).then_inc(s_text, 1)
                    wait(pool, s_vrep_in[p], 16 * i)
                    pool.tensor_tensor(v_diag[p][0:NIP * H, :], vrep[p][:, :], ipmask_sb[:, :],
                                       ALU.mult).then_inc(s_vdiag, 1)
                if has(w, lag=1):
                    wait(pool, s_max, G * b)
                    wait(pool, s_fuse, 3 * (b - 2) + 2)
                    pool.tensor_tensor(ip_stage[:, :, :], ip_score[n][:, :, :],
                                       one[:, 0:1].unsqueeze(2).broadcast_to([S, H, NIP]), ALU.mult).then_inc(s_ipstage, 1)
                if has(w) and has(w, ahead=2):
                    wait(pool, s_ctx_mm, b + 1)
                    pool.tensor_copy(ctxT_sb[p][:, :, T:TOK],
                                     ipunitT[:, :, bass.ds((b + 2) * NIP, NIP)]).then_inc(s_ipcol, 1)
                if has(w, lag=2):
                    wait(pool, s_ipmax, b - 1)
                    pool.tensor_tensor(centred[:, :, :], fused[:, :, :],
                                       ipmax[:, :].unsqueeze(2).broadcast_to([S, H, NIP]), ALU.subtract).then_inc(s_fuse, 1)
                    wait(pool, s_ipexp, b - 1)
                    pool.tensor_tensor(half[:, :, :], ip_exp[:, :, 0:2], ip_exp[:, :, 2:4], ALU.add).then_inc(s_ipsum, 1)
                    wait(pool, s_ipsum, 2 * (b - 2) + 1)
                    pool.tensor_tensor(ipsum[:, :], half[:, :, 0], half[:, :, 1], ALU.add).then_inc(s_ipsum, 1)
                if has(w, ahead=1):
                    wait(pool, s_khi, b + 2)
                    wait(pool, s_main, NPAIR * b)
                    r = main_rhs[n]
                    vs = v_stage[:, :].rearrange("t (r a d) -> t r a d", a=2, d=D)
                    ones = one[0:T, 0:1].unsqueeze(2).broadcast_to([T, NPAIR, D])
                    pool.tensor_tensor(r[:, :, 0:D], vs[:, :, 0, :], ones, ALU.mult)
                    pool.tensor_tensor(r[:, :, RW - D:RW], vs[:, :, 1, :], ones, ALU.mult).then_inc(s_vcopy, 1)
                if has(w, lag=2):
                    wait(pool, s_rip, b - 1)
                    pool.tensor_tensor(rip_masked[:, :], rip[:, :], smask_sb[:, 0:1].broadcast_to([S, H]),
                                       ALU.mult).then_inc(s_ipprobs, 1)
                    wait(pool, s_ipprobs, 2 * (b - 2) + 1)
                    wait(pool, s_pipT_mm, b - 2)
                    pool.tensor_tensor(ip_probs[:, :, :], ip_exp[:, :, :],
                                       rip_masked[:, :].unsqueeze(2).broadcast_to([S, H, NIP]), ALU.mult).then_inc(s_ipprobs, 1)
                if has(w, lag=1):
                    wait(pool, s_stats, 3 * b)
                    pool.tensor_tensor(rnorm[:, :], clamped[:, :], exponent[:, :], ALU.pow).then_inc(s_rnorm, 1)

            windows(pool, window)

        @block.scalar
        def _(act):
            def window(b, p, i, w):
                n = 1 - p
                for g in range(G):
                    grp = b * G + g
                    if g == 2 and has(w, lag=2):
                        wait(act, s_fuse, 3 * (b - 1))
                        wait(act, s_ipprobs, 2 * (b - 2))
                        act.activation(ip_exp[:, :, :], centred[:, :, :], ACT.Exp).then_inc(s_ipexp, 1)
                    if has_group(w, g, 2):
                        t = grp - 2
                        tp = (p * G + g) % 2
                        wait(act, s_transp, t + 1)
                        wait(act, s_main, PG * t - PG)
                        act.activation(probsT[tp][:, :, :].rearrange("t h s -> t (h s)"), probsT_ps[tp][0:T, :],
                                       ACT.Copy).then_inc(s_probsT, 1)
                    if g == 0 and has(w, ahead=1):
                        wait(act, s_ctx_mm, b + 2)
                        if w is None or w >= 0:
                            wait(act, s_grep[p], 16 * (i + 1))
                        act.activation(g_stage[:, NIP:NIP + TOK], pa[0:T, 0:TOK], ACT.Copy)
                        act.activation(g_stage[:, 0:NIP], pa[0:T, T:TOK], ACT.Copy).then_inc(s_gstage, 1)
                        wait(act, s_vcopy, b + 1)
                        act.activation(v_stage[:, :], pa[0:T, TOK:TOK + C], ACT.Copy)
                        act.activation(k_split[0:T, :, :, 0, :].bitcast(F32R), doubled(pa[0:T, TOK + C:TOK + 2 * C]),
                                       ACT.Copy).then_inc(s_khi, 1)
                    if g == 1 and has(w, ahead=1):
                        wait(act, s_q_mm, b + 2)
                        act.activation(q_split[:, :, 0, :, :].bitcast(F32R), doubled(pb[:, 0:C]),
                                       ACT.Copy).then_inc(s_qhi, 1)
                    if g == 1 and has(w, ahead=1):
                        wait(act, s_kT, b + 2)
                        if w is None or w >= 0:
                            wait(act, s_kd03[p], 64 * (i + 1))
                            wait(act, s_kd4[p], 64 * (i + 1))
                        act.activation(k_stack[:, 0:G - 1, :].rearrange("r g t -> r (g t)"), pa[:, :],
                                       ACT.Copy).then_inc(s_kst03, 1)
                    if g == 3 and has(w, ahead=1):
                        wait(act, s_kq4, b + 2)
                        act.activation(k_stack[:, G - 1, :], pb[:, 0:TOK], ACT.Copy)
                        act.activation(q_stack[n][:, G - 1, :], pb[:, TOK:TOK + S], ACT.Copy).then_inc(s_st4, 1)
                    if has(w):
                        act.wait_ge(s_max, grp + 1)
                        for j in range(HG):
                            h = HG * g + j
                            last = act.activation(probs[p][:, h, :], score_ps[(p * G + g) % 2][:, j * TOK:j * TOK + T],
                                                  ACT.Exp, bias=negmax[p][:, h:h + 1])
                        last.then_inc(s_exp, 1)
                    if g == 3 and has(w, ahead=1):
                        wait(act, s_qT, b + 2)
                        act.activation(q_stack[n][:, 0:G - 1, :].rearrange("r g t -> r (g t)"), pa[:, :],
                                       ACT.Copy).then_inc(s_qst03, 1)

            windows(act, window)

        @block.vector
        def _(dve):
            for p in range(2):
                last = dve.memset(k_diag[p][:, :, :, :].bitcast(F32), 0.0)
            last.then_inc(s_ipv, 1)
            dve.wait_ge(s_ipp, 1)
            kips = doubled(pa[0:B * NIP, 0:C])
            dve.tensor_copy(kip_split[:, :, :, 0, :].bitcast(F32R), kips).then_inc(s_klo, 1)
            dve.wait_ge(s_klo, 1)
            dve.tensor_tensor(kip_split[:, :, :, 1, :].bitcast(F32R), kips, kip_split[:, :, :, 0, :],
                              ALU.subtract).then_inc(s_ipv, 1)
            dve.tensor_copy(vip_sb[:, :], pa[0:B * NIP, C:2 * C]).then_inc(s_ipv, 1)
            dve.wait_ge(s_ipin, 16 * 4)
            dve.tensor_tensor_reduce(ip_junk[:, :], ip_sb[:, :], ip_sb[:, :], 1.0, 0.0, ALU.mult, ALU.add,
                                     ip_ss[:, 0:1]).then_inc(s_ipv, 1)
            dve.wait_ge(s_ipv, 4)
            dve.tensor_scalar(ip_ss[:, 1:2], ip_ss[:, 0:1], EPS2, None, ALU.max).then_inc(s_ipv, 1)
            dve.wait_ge(s_iprn, 1)
            dve.tensor_scalar(ipunit[:, :], ip_sb[:, :], ip_ss[:, 2:3], 0.5, ALU.mult, ALU.mult).then_inc(s_ipv, 1)
            dve.wait_ge(s_ipp, 2)
            dve.tensor_copy(ipunitT[:, :, :].rearrange("p c t -> p (c t)"), pb[:, 0:EC * B * NIP]).then_inc(s_ipv, 2)
            dve.wait_ge(s_init, 2)

            def window(b, p, i, w):
                n = 1 - p
                for g in range(G):
                    grp = b * G + g
                    if g == 0 and has(w, lag=3):
                        wait(dve, s_pipT_mm, b - 2)
                        dve.tensor_copy(ip_probsT[0:NIP * H, :], pb[0:NIP * H, 0:S]).then_inc(s_pipT, 1)
                    if g == 1 and has(w, ahead=1):
                        wait(dve, s_khi, b + 2)
                        dve.tensor_tensor(k_split[0:T, :, :, 1, :].bitcast(F32R), doubled(pa[0:T, TOK + C:TOK + 2 * C]),
                                          k_split[0:T, :, :, 0, :], ALU.subtract).then_inc(s_klo, 1)
                    if g == 1 and has(w, lag=3):
                        wait(dve, s_outT_mm, b - 2)
                        dve.tensor_copy(oT[0:CH, :, :].rearrange("c a s -> c (a s)"), pb[0:CH, 0:2 * S]).then_inc(s_oT, 1)
                    if g == 2 and has(w, ahead=1):
                        wait(dve, s_qhi, b + 2)
                        dve.tensor_tensor(q_split[:, :, 1, :, :].bitcast(F32R), doubled(pb[:, 0:C]),
                                          q_split[:, :, 0, :, :], ALU.subtract).then_inc(s_qlo, 1)
                    if g == 4 and has(w, lag=2):
                        wait(dve, s_ipsum, 2 * (b - 1))
                        wait(dve, s_ipprobs, 2 * (b - 2))
                        dve.reciprocal(rip[:, :], ipsum[:, :]).then_inc(s_rip, 1)
                    if g == 4 and has(w, lag=1):
                        den = bass.AP(small[n], NIP, [[NPAIR * SMALL, S], [SMALL, NPAIR], [2 * D + 1, 2]])
                        wait(dve, s_norm, NPAIR * b)
                        wait(dve, s_text, b - 1)
                        wait(dve, s_rnorm, b - 1)
                        dve.scalar_tensor_tensor(out=guard[:, :].rearrange("s (r a) -> s r a", a=2), in0=den, scalar=EPS2,
                                                 in1=den, op0=ALU.mult, op1=ALU.mult).then_inc(s_stats, 1)
                        dve.reciprocal(rden[:, :].rearrange("s (r a) -> s r a", a=2), den).then_inc(s_stats, 1)
                        wait(dve, s_stats, 3 * (b - 1) + 1)
                        dve.tensor_tensor(clamped[:, :], norm2[n][:, :], guard[:, :], ALU.max).then_inc(s_stats, 1)
                    if has_group(w, g, 4):
                        wb = p if g >= 4 else n
                        gg = (g - 4) % G
                        if gg == 0:
                            wait(dve, s_text, b - 1)
                        for r in range(PG):
                            pair = grp * PG + r - 4 * PG
                            wait(dve, s_norm, pair - 1)
                            wait(dve, s_main, pair + 1)
                            for a in range(2):
                                h = HG * gg + 2 * r + a
                                u = main_ps[r][:, a * (T + SMALL):a * (T + SMALL) + T]
                                dve.tensor_tensor_reduce(junk[:, 2 * r + a, :], u, probs[wb][:, h, :], 1.0, 0.0, ALU.mult,
                                                         ALU.add, norm2[wb][:, h:h + 1])
                            dve.tensor_copy(small[wb][:, PG * gg + r, :],
                                            main_ps[r][:, T:T + SMALL]).then_inc(s_norm, 1)
                    if g == 3 and has(w, lag=3):
                        wait(dve, s_final_mm, b - 2)
                        wait(dve, s_xn_in[n], 16 * (i - 1 + p))
                        wait(dve, s_store[n], 16 * (i - 2 + p))
                        dve.tensor_tensor(out_sb[n][:, :], pb[:, 0:C], xn_sb[n][:, :], ALU.add).then_inc(s_final, 1)
                    if has(w):
                        wait(dve, s_scores, grp + 1)
                        if g == 0:
                            wait(dve, s_ipstage, b - 1)
                        sc = score_ps[(p * G + g) % 2][:, :].rearrange("s (h t) -> s h t", t=TOK)
                        dve.tensor_copy(ip_score[p][:, HG * g:HG * g + HG, :], sc[:, :, T:TOK])
                        dve.tensor_reduce(negmax[p][:, HG * g:HG * g + HG], sc[:, :, 0:T], AX_X, ALU.max,
                                          negate=True).then_inc(s_max, 1)
                    if g == 1 and has(w, lag=2):
                        wait(dve, s_fuse, 3 * (b - 2) + 2)
                        dve.tensor_reduce(ipmax[:, :], fused[:, :, :], AX_X, ALU.max).then_inc(s_ipmax, 1)

            windows(dve, window)

        @block.tensor
        def _(pe):
            pe.wait_ge(s_ipin, 16 * 4)
            for c in range(EC):
                mm = pe.matmul(pa[0:B * NIP, 0:2 * C], ipT_sb[:, c, :], wkvip_sb[:, c, :], start=(c == 0), stop=(c == EC - 1))
            mm.then_inc(s_ipp, 1)
            pe.wait_ge(s_ipv, 6)
            for c in range(EC):
                mm = pe.transpose(pb[:, c * B * NIP:(c + 1) * B * NIP], ipunit[:, c * 128:(c + 1) * 128],
                                  ident_sb[0:B * NIP, 0:B * NIP])
            mm.then_inc(s_ipp, 1)
            pe.wait_ge(s_ipv, 8)
            pe.wait_ge(s_const, 16 * 5)
            pe.wait_ge(s_init, 4)

            def stacked(split, g):
                return split[:, HG * g:HG * g + HG, :, :, :].rearrange("t h a b d -> t (h a b d)")

            def window(b, p, i, w):
                n = 1 - p
                for g in range(G):
                    grp = b * G + g
                    if has(w):
                        if g == 0:
                            wait(pe, s_kd03[p], 64 * (i + 1))
                            wait(pe, s_qst03, b + 1)
                        if g == G - 1:
                            wait(pe, s_kd4[p], 64 * (i + 1))
                        wait(pe, s_exp, grp - 1)
                        pe.matmul(score_ps[(p * G + g) % 2][:, :], q_stack[p][:, g, :],
                                  k_diag[p][:, g, :, :].rearrange("r h t -> r (h t)"), start=True,
                                  stop=True).then_inc(s_scores, 1)
                    if has_group(w, g, 2):
                        tg, tb = (g - 2) % G, (p if g >= 2 else n)
                        tp = (p * G + g) % 2
                        wait(pe, s_exp, grp - 1)
                        wait(pe, s_probsT, grp - 3)
                        for j in range(HG):
                            mm = pe.transpose(probsT_ps[tp][0:T, j * S:(j + 1) * S], probs[tb][:, HG * tg + j, :],
                                              ident_sb[:, :])
                        mm.then_inc(s_transp, 1)
                    if g == 0 and has(w, ahead=1):
                        wait(pe, s_ctx_in[n], 16 * (i + p + 1))
                        wait(pe, s_ipcol, b + 2)
                        wait(pe, s_qst03, b + 1)
                        for lo, width, rhs in ((0, TOK, None), (TOK, C, 0), (TOK + C, C, C)):
                            for c in range(EC):
                                r = ctxT_sb[n][:, c, :] if rhs is None else wkv_sb[:, c, rhs:rhs + C]
                                mm = pe.matmul(pa[:, lo:lo + width], ctxT_sb[n][:, c, :], r, start=(c == 0), stop=(c == EC - 1))
                        mm.then_inc(s_ctx_mm, 1)
                    if g == 1 and has(w, ahead=1):
                        wait(pe, s_xT_in[n], 16 * (i + p + 1))
                        wait(pe, s_oT, b - 2)
                        wait(pe, s_st4, b + 1)
                        for c in range(2):
                            mm = pe.matmul(pb[:, 0:C], xT_sb[n][:, c, :], wq_scaled[:, c, :], start=(c == 0), stop=(c == 1))
                        mm.then_inc(s_q_mm, 1)
                    if g == 3 and has(w, ahead=1):
                        wait(pe, s_final, b - 2)
                        wait(pe, s_qlo, b + 2)
                        pe.transpose(pb[:, 0:TOK], stacked(k_split, G - 1), ident_sb[:, :])
                        pe.transpose(pb[:, TOK:TOK + S], stacked(q_split, G - 1), ident_sb[:, :]).then_inc(s_kq4, 1)
                    if g == 3 and has(w, ahead=1):
                        wait(pe, s_qlo, b + 2)
                        wait(pe, s_kst03, b + 2)
                        for k in range(G - 1):
                            mm = pe.transpose(pa[:, k * S:(k + 1) * S], stacked(q_split, k), ident_sb[:, :])
                        mm.then_inc(s_qT, 1)
                    if has_group(w, g, 3):
                        mg, mb = (g - 3) % G, (p if g >= 3 else n)
                        mp = (p * G + g - 3) % 2
                        if mg == 0:
                            wait(pe, s_grep[mb], 16 * (i + 1))
                            wait(pe, s_vcopy, b + 1)
                        wait(pe, s_probsT, grp - 2)
                        for r in range(PG):
                            pair = grp * PG + r - 3 * PG
                            wait(pe, s_norm, pair - 1)
                            blk = main_rhs[mb][:, PG * mg + r, :]
                            pe.matmul(main_ps[r][:, 0:MAIN], probsT[mp][:, 2 * r, :], blk[:, RW - MAIN:RW],
                                      start=True, stop=True)
                            pe.matmul(main_ps[r][:, MAIN:2 * MAIN], probsT[mp][:, 2 * r + 1, :], blk[:, 0:MAIN],
                                      start=True, stop=True).then_inc(s_main, 1)
                    if g == 0 and has(w, lag=3):
                        wait(pe, s_pipT, b - 2)
                        wait(pe, s_text, b - 2)
                        wait(pe, s_vdiag, b - 2)
                        for c in range(2):
                            pe.matmul(pb[0:CH, c * S:(c + 1) * S], text[:, c * CH:(c + 1) * CH], ident_sb[:, :],
                                      start=True, stop=False)
                            mm = pe.matmul(pb[0:CH, c * S:(c + 1) * S], v_diag[n][:, c * CH:(c + 1) * CH], ip_probsT[:, :],
                                           start=False, stop=True)
                        mm.then_inc(s_outT_mm, 1)
                    if g == 1 and has(w, ahead=1):
                        wait(pe, s_klo, b + 3)
                        wait(pe, s_kip_in, 16 * (b + 2))
                        for k in range(G - 1):
                            mm = pe.transpose(pa[:, k * TOK:(k + 1) * TOK], stacked(k_split, k), ident_sb[:, :])
                        mm.then_inc(s_kT, 1)
                    if g == 2 and has(w, lag=3):
                        wait(pe, s_oT, b - 2)
                        if has(w, ahead=1):
                            wait(pe, s_qlo, b + 2)
                        for c in range(2):
                            mm = pe.matmul(pb[:, 0:C], oT[:, c, :], wout_sb[:, c, :], start=(c == 0), stop=(c == 1))
                        mm.then_inc(s_final_mm, 1)
                    if g == 4 and has(w, lag=2):
                        wait(pe, s_ipprobs, 2 * (b - 1))
                        wait(pe, s_final, b - 2)
                        if has(w, ahead=1):
                            wait(pe, s_st4, b + 2)
                        pe.transpose(pb[0:NIP * H, 0:S], ip_probs[:, :, :].rearrange("s h m -> s (h m)"),
                                     ident_sb[:, :]).then_inc(s_pipT_mm, 1)

            windows(pe, window)


def kernel(x, ctx_2048, fside_S_0, L0_xattn_W_q, L0_xattn_W_k, L0_xattn_W_v, L0_xattn_W_k_ip, L0_xattn_W_v_ip,
           L0_xattn_W_out, L0_xattn_b_out):
    import numpy as np
    import concourse.bacc as bacc
    from concourse.bass_utils import run_bass_kernel_spmd

    def chunks(a, n):
        return np.ascontiguousarray(np.moveaxis(a.reshape(n, a.shape[0] // n, *a.shape[1:]), 0, 1))

    x = np.asarray(x)
    cx = np.asarray(ctx_2048)
    wk, wv, wkip, wvip = (np.asarray(a) for a in (L0_xattn_W_k, L0_xattn_W_v, L0_xattn_W_k_ip, L0_xattn_W_v_ip))
    wv_swapped = wv.reshape(E, NPAIR, 2, D)[:, :, ::-1].reshape(E, C)
    wout = np.asarray(L0_xattn_W_out)
    wout_rows = np.zeros((CH + 1, 2, C), np.float32)
    wout_rows[:CH] = chunks(wout, 2)
    wout_rows[CH, 1] = np.asarray(L0_xattn_b_out)
    ip = np.ascontiguousarray(cx[:, T:].reshape(B * NIP, E))
    ipmask = np.zeros((H, NIP, H, D), np.float32)
    for h in range(H):
        ipmask[h, :, h] = 1.0
    arrays = {
        "xT": np.ascontiguousarray(x.reshape(B, S, 2, CH).transpose(0, 3, 2, 1)),
        "xn": np.ascontiguousarray(x),
        "ctxT": np.ascontiguousarray(cx[:, :T].reshape(B, T, EC, 128).transpose(0, 3, 2, 1)),
        "ipT": np.ascontiguousarray(ip.reshape(B * NIP, EC, 128).transpose(2, 1, 0)),
        "ipn": ip,
        "smask": np.ascontiguousarray(np.asarray(fside_S_0).reshape(S, 1)),
        "wq": chunks(np.asarray(L0_xattn_W_q), 2),
        "wkv": chunks(np.concatenate([wv_swapped, wk], 1), EC),
        "wkvip": chunks(np.concatenate([wkip, wvip], 1), EC),
        "wout": wout_rows,
        "ident": np.eye(128, dtype=np.float32),
        "ipmask": ipmask.reshape(H * NIP, C),
    }
    nc = bacc.Bacc("TRN2", target_bir_lowering=False, num_devices=1)
    args = {name: nc.dram_tensor(name, a.shape, mybir.dt.from_np(a.dtype), kind="ExternalInput").ap()
            for name, a in arrays.items()}
    kip_d = nc.dram_tensor("kip_d", (B * NIP, 4 * C), F32, kind="Internal").ap()
    vip_d = nc.dram_tensor("vip_d", (B * NIP, C), F32, kind="Internal").ap()
    out = nc.dram_tensor("out", (B, S, C), F32, kind="ExternalOutput").ap()
    xattn_program(nc, **args, kip_d=kip_d, vip_d=vip_d, out=out)
    r = run_bass_kernel_spmd(nc, [arrays], core_ids=[0])
    return r.results[0]["out"]
```

```python
from contextlib import ExitStack

import concourse.bass as bass
from concourse import mybir

F32 = mybir.dt.float32
F32R = mybir.dt.float32r
ALU = mybir.AluOpType
ACT = mybir.ActivationFunctionType
AX_X = mybir.AxisListType.X

B, S, C = 16, 128, 160
H, D = 20, 8
T, NIP, E = 124, 4, 256
TOK = T + NIP
EC = E // 128
CH = C // 2
CP = 96
HG = 4
G = H // HG
PG = HG // 2
NPAIR = H // 2
PARTED = 3
SCALE = float(D) ** -0.5
EPS2 = 1e-24
MAIN = D + 1 + NIP + T
SMALL = 2 * (D + 1 + NIP)
RW = SMALL + T
BANK = 512


def xattn_program(nc, xT, xn, ctxT, ipT, ipn, smask, wq, wkv, wkvip, wout, ident, kip_d, vip_d, out):
    with ExitStack() as ctx:
        def sb(name, shape, dt=F32):
            return ctx.enter_context(nc.sbuf_tensor(name, shape, dt))

        def sem(name):
            return ctx.enter_context(nc.semaphore(name))

        def two(make, name, *a):
            return [make(f"{name}{p}", *a) for p in range(2)]

        wq_sb = sb("wq_sb", [CP, 2, C])
        wq_scaled = sb("wq_scaled", [CP, 2, C])
        wkv_sb = sb("wkv_sb", [128, EC, 2 * C])
        wkvip_sb = sb("wkvip_sb", [128, EC, 2 * C])
        wout_sb = sb("wout_sb", [CP, 2, C])
        ident_sb = sb("ident_sb", [128, 128])
        ident_r_sb = sb("ident_r_sb", [128, 128], F32R)
        smask_sb = sb("smask_sb", [S, 1])
        ipT_sb = sb("ipT_sb", [128, EC, B * NIP])
        ip_sb = sb("ip_sb", [B * NIP, E])
        ip_junk = sb("ip_junk", [B * NIP, E])
        ip_ss = sb("ip_ss", [B * NIP, 3])
        ipunit = sb("ipunit", [B * NIP, E])
        ipunitT = sb("ipunitT", [128, EC, B * NIP])
        kip_split = sb("kip_split", [B * NIP, H, 2, 2, D])
        vip_sb = sb("vip_sb", [B * NIP, C])
        xT_sb = two(sb, "xT_sb", [CP, 2, S])
        xn_sb = two(sb, "xn_sb", [S, C])
        ctxT_sb = two(sb, "ctxT_sb", [128, EC, TOK])
        g_stage = sb("g_stage", [T, NIP + TOK])
        v_stage = sb("v_stage", [T, C])
        k_split = sb("k_split", [TOK, H, 2, 2, D], F32R)
        q_split = sb("q_split", [S, H, 2, 2, D], F32R)
        k_stack = sb("k_stack", [128, G, TOK])
        q_stack = two(sb, "q_stack", [128, G, S], F32R)
        k_diag = two(sb, "k_diag", [128, G, HG, TOK], F32R)
        main_rhs = two(sb, "main_rhs", [T, NPAIR, RW])
        negmax = two(sb, "negmax", [S, H])
        probs = two(sb, "probs", [S, H, T])
        probsT = two(sb, "probsT", [T, HG, S])
        norm2 = two(sb, "norm2", [S, H])
        small = two(sb, "small", [S, NPAIR, SMALL])
        ip_score = two(sb, "ip_score", [S, H, NIP])
        junk = sb("junk", [S, 2 * PG, T])
        one = sb("one", [128, 1])
        exponent = sb("exponent", [S, H])
        guard = sb("guard", [S, H])
        clamped = sb("clamped", [S, H])
        rnorm = sb("rnorm", [S, H])
        rden = sb("rden", [S, H])
        ip_stage = sb("ip_stage", [S, H, NIP])
        fused = sb("fused", [S, H, NIP])
        centred = sb("centred", [S, H, NIP])
        ip_exp_half = sb("ip_exp_half", [S, H, 2])
        ipmax = sb("ipmax", [S, H])
        ip_exp = sb("ip_exp", [S, H, NIP])
        ipsum = sb("ipsum", [S, H])
        rip = sb("rip", [S, H])
        rip_masked = sb("rip_masked", [S, H])
        ip_probs = sb("ip_probs", [S, H, NIP])
        text = two(sb, "text", [S, C])
        vrep = two(sb, "vrep", [S, NIP, H, D])
        ip_prod = sb("ip_prod", [S, NIP, H, D])
        ip_half = sb("ip_half", [S, 2, C])
        ip_out = sb("ip_out", [S, C])
        attn_out = sb("attn_out", [S, C])
        oT = sb("oT", [CP, 2, S])
        out_sb = two(sb, "out_sb", [S, C])

        def bank(name):
            return ctx.enter_context(nc.psum_tensor(name, [128, BANK], F32))

        score_ps = two(bank, "score_ps")
        probsT_ps = two(bank, "probsT_ps")
        main_ps = two(bank, "main_ps")
        pa = bank("pa")
        pb = bank("pb")

        s_ipn_in = sem("s_ipn_in")
        s_ident_in = sem("s_ident_in")
        s_ipw_in = sem("s_ipw_in")
        s_wkv_in = sem("s_wkv_in")
        s_wq_in = sem("s_wq_in")
        s_const_in = sem("s_const_in")
        s_kip_out = sem("s_kip_out")
        s_vip_out = sem("s_vip_out")
        s_ctx_in = two(sem, "s_ctx_in")
        s_xT_in = two(sem, "s_xT_in")
        s_xn_in = two(sem, "s_xn_in")
        s_vrep_in = two(sem, "s_vrep_in")
        s_kip_in = sem("s_kip_in")
        s_grep = two(sem, "s_grep")
        s_kd03 = two(sem, "s_kd03")
        s_kd4 = two(sem, "s_kd4")
        s_store = two(sem, "s_store")
        s_fill = sem("s_fill")
        s_zeros = two(sem, "s_zeros")
        s_ipnorm = sem("s_ipnorm")
        s_iprn = sem("s_iprn")
        s_ipunit = sem("s_ipunit")
        s_ipunit_T = sem("s_ipunit_T")
        s_ipunitT = sem("s_ipunitT")
        s_ipk_mm = sem("s_ipk_mm")
        s_kip = sem("s_kip")
        s_ipv_mm = sem("s_ipv_mm")
        s_vip = sem("s_vip")
        s_wq = sem("s_wq")
        s_ctx_mm = sem("s_ctx_mm")
        s_q_mm = sem("s_q_mm")
        s_kT = sem("s_kT")
        s_kq4 = sem("s_kq4")
        s_qT = sem("s_qT")
        s_scores = sem("s_scores")
        s_transp = sem("s_transp")
        s_main = sem("s_main")
        s_oT_tr = sem("s_oT_tr")
        s_final_mm = sem("s_final_mm")
        s_gstage = sem("s_gstage")
        s_khi = sem("s_khi")
        s_qhi = sem("s_qhi")
        s_kst03 = sem("s_kst03")
        s_st4 = sem("s_st4")
        s_qst03 = sem("s_qst03")
        s_exp = sem("s_exp")
        s_probsT = sem("s_probsT")
        s_ipexp = sem("s_ipexp")
        s_klo = sem("s_klo")
        s_qlo = sem("s_qlo")
        s_max = sem("s_max")
        s_norm = sem("s_norm")
        s_stats = sem("s_stats")
        s_ipmax = sem("s_ipmax")
        s_rip = sem("s_rip")
        s_attn = sem("s_attn")
        s_oT = sem("s_oT")
        s_final = sem("s_final")
        s_ipcol = sem("s_ipcol")
        s_vcopy = sem("s_vcopy")
        s_rnorm = sem("s_rnorm")
        s_ipstage = sem("s_ipstage")
        s_fuse = sem("s_fuse")
        s_centred = sem("s_centred")
        s_ipsum = sem("s_ipsum")
        s_ipprobs = sem("s_ipprobs")
        s_text = sem("s_text")
        s_ipout = sem("s_ipout")

        block = ctx.enter_context(nc.Block())

        def doubled(cols):
            r = cols.rearrange("t (h d) -> t h d", d=D)
            return r.unsqueeze(2).broadcast_to([r.shape[0], H, 2, D])

        def windows(eng, window):
            for w in range(-1, 4):
                window(w, w % 2, w // 2, w)
            with eng.Fori(2, B // 2 - 1) as i:
                for p in range(2):
                    window(i * 2 + p, p, i, None)
            for w in range(B - 2, B + 3):
                window(w, w % 2, w // 2, w)

        def has(w, lag=0, ahead=0):
            return w is None or 0 <= w - lag + ahead < B

        def has_group(w, g, lag):
            return w is None or 0 <= G * w + g - lag < G * B

        def wait(eng, s, value):
            if isinstance(value, int) and value <= 0:
                return
            eng.wait_ge(s, value)

        def ip_output(eng, b, p, i):
            n = 1 - p
            wait(eng, s_vrep_in[n], 16 * (i - 1 + p))
            wait(eng, s_ipprobs, 2 * (b - 2))
            wait(eng, s_ipout, 3 * (b - 3))
            eng.tensor_tensor(ip_prod[:, :, :, :], vrep[n][:, :, :, :],
                               ip_probs[:, :, :].rearrange("s h m -> s m h").unsqueeze(3).broadcast_to([S, NIP, H, D]),
                               ALU.mult).then_inc(s_ipout, 1)
            r = ip_prod[:, :, :, :].rearrange("s m h d -> s m (h d)")
            wait(eng, s_ipout, 3 * (b - 3) + 1)
            eng.tensor_tensor(ip_half[:, :, :], r[:, 0:2, :], r[:, 2:4, :], ALU.add).then_inc(s_ipout, 1)
            wait(eng, s_ipout, 3 * (b - 3) + 2)
            wait(eng, s_attn, b - 3)
            eng.tensor_tensor(ip_out[:, :], ip_half[:, 0, :], ip_half[:, 1, :], ALU.add).then_inc(s_ipout, 1)

        @block.sync
        def _(sp):
            sp.dma_start(ip_sb[:, :], ipn).then_inc(s_ipn_in, 16)
            sp.dma_start(ipT_sb[:, :, :], ipT).then_inc(s_ipw_in, 16)
            sp.dma_start(wkvip_sb[:, :, :], wkvip).then_inc(s_ipw_in, 16)
            sp.dma_start(ident_sb[:, :], ident).then_inc(s_ident_in, 16)
            sp.dma_start(wkv_sb[:, :, :], wkv).then_inc(s_wkv_in, 16)
            sp.dma_start(ctxT_sb[0][:, :, 0:T], ctxT[0]).then_inc(s_ctx_in[0], 16)
            sp.wait_ge(s_fill, 1)
            sp.dma_start(wq_sb[0:CH, :, :], wq).then_inc(s_wq_in, 16)
            sp.dma_start(xT_sb[0][0:CH, :, :], xT[0]).then_inc(s_xT_in[0], 16)
            sp.dma_start(ctxT_sb[1][:, :, 0:T], ctxT[1]).then_inc(s_ctx_in[1], 16)
            sp.dma_start(xT_sb[1][0:CH, :, :], xT[1]).then_inc(s_xT_in[1], 16)
            sp.wait_ge(s_kip, 2)
            sp.dma_start(k_split[T:TOK, :, :, :, :].rearrange("t h c a d -> t (h c a d)").bitcast(F32),
                         kip_split[0:NIP, :, :, :, :].rearrange("t h c a d -> t (h c a d)")).then_inc(s_kip_in, 16)
            sp.dma_start(kip_d, kip_split[:, :, :, :, :].rearrange("t h c a d -> t (h c a d)")).then_inc(s_kip_out, 16)
            sp.wait_ge(s_vip, 1)
            sp.dma_start(vip_d, vip_sb[:, :]).then_inc(s_vip_out, 16)
            sp.dma_start(smask_sb[:, :], smask).then_inc(s_const_in, 16)
            sp.dma_start(wout_sb[0:CH + 1, :, :], wout).then_inc(s_const_in, 16)
            sp.wait_ge(s_fill, 3)
            sp.wait_ge(s_kip_out, 16)
            sp.wait_ge(s_vip_out, 16)
            sp.wait_ge(s_zeros[1], 1)

            def window(b, p, i, w):
                n = 1 - p
                if has(w) and has(w, ahead=1):
                    wait(sp, s_kT, b + 1)
                    wait(sp, s_kq4, b + 1)
                    sp.dma_start(k_split[T:TOK, :, :, :, :].rearrange("t h c a d -> t (h c a d)").bitcast(F32),
                                 kip_d[bass.ds((b + 1) * NIP, NIP), :]).then_inc(s_kip_in, 16)
                if has(w) and has(w, ahead=2):
                    wait(sp, s_ctx_mm, b + 1)
                    sp.dma_start(ctxT_sb[p][:, :, 0:T], ctxT[b + 2]).then_inc(s_ctx_in[p], 16)
                    wait(sp, s_q_mm, b + 1)
                    sp.dma_start(xT_sb[p][0:CH, :, :], xT[b + 2]).then_inc(s_xT_in[p], 16)
                if has(w, lag=2):
                    wait(sp, s_final, b - 3)
                    sp.dma_start(xn_sb[p][:, :], xn[b - 2]).then_inc(s_xn_in[p], 16)
                    wait(sp, s_ipout, 3 * (b - 4) + 1)
                    sp.dma_start(vrep[p][:, :, :, :].rearrange("s m h d -> s (m h d)"),
                                 bass.AP(vip_d.tensor, vip_d.offset + (b - 2) * (NIP * C),
                                         [[0, S], [1, NIP * C]])).then_inc(s_vrep_in[p], 16)
                if has(w, ahead=1):
                    wait(sp, s_scores, G * b)
                    wait(sp, s_kst03, b + 2)
                    for j in range(HG if w != -1 else 0):
                        sp.dma_start(k_diag[n][32 * j:32 * j + 32, 0:G - 1, j, :].bitcast(F32),
                                     k_stack[32 * j:32 * j + 32, 0:G - 1, :]).then_inc(s_kd03[n], 16)
                    wait(sp, s_main, NPAIR * b)
                    wait(sp, s_gstage, b + 2)
                    sp.dma_start(main_rhs[n][:, :, D + 1:D + 1 + NIP + TOK],
                                 g_stage[:, :].unsqueeze(1).broadcast_to([T, NPAIR, NIP + TOK])).then_inc(s_grep[n], 16)
                    wait(sp, s_st4, b + 2)
                    for j in range(HG if w != -1 else 0):
                        sp.dma_start(k_diag[n][32 * j:32 * j + 32, G - 1, j, :].bitcast(F32),
                                     k_stack[32 * j:32 * j + 32, G - 1, :]).then_inc(s_kd4[n], 16)
                if has(w, lag=3):
                    wait(sp, s_final, b - 2)
                    sp.dma_start(out[b - 3], out_sb[n][:, :]).then_inc(s_store[n], 16)

            windows(sp, window)
            for p in range(2):
                sp.wait_ge(s_store[p], 16 * (B // 2))

        @block.gpsimd
        def _(pool):
            pool.memset(xT_sb[0][:, :, :], 0.0)
            pool.memset(xT_sb[1][:, :, :], 0.0)
            pool.memset(wq_sb[:, :, :], 0.0)
            pool.memset(wout_sb[:, :, :], 0.0).then_inc(s_fill, 1)
            pool.memset(one[:, :], 1.0)
            pool.memset(exponent[:, :], -0.5).then_inc(s_fill, 1)
            pool.memset(main_rhs[0][:, :, :], 1.0)
            pool.wait_ge(s_ipnorm, 2)
            pool.wait_ge(s_fill, 2)
            pool.tensor_tensor(ip_ss[:, 2:3], ip_ss[:, 1:2], exponent[0:B * NIP, 0:1], ALU.pow).then_inc(s_iprn, 1)
            pool.wait_ge(s_ipunitT, 1)
            for b in range(2):
                pool.tensor_copy(ctxT_sb[b][:, :, T:TOK], ipunitT[:, :, b * NIP:(b + 1) * NIP]).then_inc(s_ipcol, 1)
            pool.memset(main_rhs[1][:, :, :], 1.0)
            pool.memset(oT[:, :, :], 1.0).then_inc(s_fill, 1)
            pool.memset(k_diag[1][:, :, :, :].bitcast(F32), 0.0).then_inc(s_zeros[1], 1)
            pool.wait_ge(s_fill, 3)
            pool.wait_ge(s_const_in, 16 * 2)

            def per_head(t, width):
                return t[:, :].rearrange("s (r a) -> s r a", a=2).unsqueeze(3).broadcast_to([S, NPAIR, 2, width])

            def window(b, p, i, w):
                n = 1 - p
                num = bass.AP(small[p], 0, [[NPAIR * SMALL, S], [SMALL, NPAIR], [SMALL - NIP, 2], [1, NIP]])
                v_sum = bass.AP(small[p], NIP + 1, [[NPAIR * SMALL, S], [SMALL, NPAIR], [D, 2], [1, D]])
                if has(w, lag=2):
                    wait(pool, s_rnorm, b if w == B + 1 else b - 1)
                    pool.tensor_tensor(fused[:, :, :].rearrange("s (r a) m -> s r a m", a=2), num,
                                       per_head(rnorm, NIP), ALU.mult).then_inc(s_fuse, 1)
                    wait(pool, s_fuse, 2 * (b - 2) + 1)
                    wait(pool, s_ipstage, b - 1)
                    pool.tensor_tensor(fused[:, :, :], fused[:, :, :], ip_stage[:, :, :], ALU.add).then_inc(s_fuse, 1)
                if has(w, lag=3) and (w is None or w < B):
                    ip_output(pool, b, p, i)
                if has(w, lag=2):
                    wait(pool, s_attn, b - 3)
                    pool.tensor_tensor(text[p][:, :].rearrange("s (r a d) -> s r a d", a=2, d=D), v_sum,
                                       per_head(rden, D), ALU.mult).then_inc(s_text, 1)
                if has(w, lag=1):
                    wait(pool, s_max, G * b)
                    wait(pool, s_fuse, 2 * (b - 1))
                    pool.tensor_tensor(ip_stage[:, :, :], ip_score[n][:, :, :],
                                       one[:, 0:1].unsqueeze(2).broadcast_to([S, H, NIP]), ALU.mult).then_inc(s_ipstage, 1)
                if has(w) and has(w, ahead=2):
                    wait(pool, s_ctx_mm, b + 1)
                    pool.tensor_copy(ctxT_sb[p][:, :, T:TOK],
                                     ipunitT[:, :, bass.ds((b + 2) * NIP, NIP)]).then_inc(s_ipcol, 1)
                if has(w, lag=2):
                    wait(pool, s_ipmax, b - 1)
                    pool.tensor_tensor(centred[:, :, :], fused[:, :, :],
                                       ipmax[:, :].unsqueeze(2).broadcast_to([S, H, NIP]), ALU.subtract).then_inc(s_centred, 1)
                if has(w, lag=2):
                    wait(pool, s_ipexp, b - 1)
                    pool.tensor_tensor(ip_exp_half[:, :, :], ip_exp[:, :, 0:2], ip_exp[:, :, 2:4], ALU.add).then_inc(s_ipsum, 1)
                    wait(pool, s_ipsum, 2 * (b - 2) + 1)
                    pool.tensor_tensor(ipsum[:, :], ip_exp_half[:, :, 0], ip_exp_half[:, :, 1], ALU.add).then_inc(s_ipsum, 1)
                if has(w, ahead=1):
                    wait(pool, s_khi, b + 2)
                    wait(pool, s_main, NPAIR * b)
                    r = main_rhs[n]
                    vs = v_stage[:, :].rearrange("t (r a d) -> t r a d", a=2, d=D)
                    ones = one[0:T, 0:1].unsqueeze(2).broadcast_to([T, NPAIR, D])
                    pool.tensor_tensor(r[:, :, 0:D], vs[:, :, 0, :], ones, ALU.mult)
                    pool.tensor_tensor(r[:, :, RW - D:RW], vs[:, :, 1, :], ones, ALU.mult).then_inc(s_vcopy, 1)
                if w == B:
                    heads = slice(0, HG * PARTED)
                    wait(pool, s_stats, 3 * b)
                    pool.tensor_tensor(rnorm[:, heads], clamped[:, heads], exponent[:, heads], ALU.pow).then_inc(s_rnorm, 1)
                if has(w, lag=2):
                    wait(pool, s_rip, b - 1)
                    pool.tensor_tensor(rip_masked[:, :], rip[:, :], smask_sb[:, 0:1].broadcast_to([S, H]),
                                       ALU.mult).then_inc(s_ipprobs, 1)
                    wait(pool, s_ipprobs, 2 * (b - 2) + 1)
                    wait(pool, s_ipout, 3 * (b - 3) + 1)
                    pool.tensor_tensor(ip_probs[:, :, :], ip_exp[:, :, :],
                                       rip_masked[:, :].unsqueeze(2).broadcast_to([S, H, NIP]), ALU.mult).then_inc(s_ipprobs, 1)
                if has(w, lag=1):
                    heads = slice(HG * PARTED if w == B else 0, H)
                    wait(pool, s_stats, 3 * b + 3 if w == B else 3 * b)
                    pool.tensor_tensor(rnorm[:, heads], clamped[:, heads], exponent[:, heads], ALU.pow).then_inc(s_rnorm, 1)

            windows(pool, window)

        @block.scalar
        def _(act):
            def window(b, p, i, w):
                n = 1 - p
                for g in range(G):
                    grp = b * G + g
                    if g == 0 and has(w, ahead=1):
                        wait(act, s_ctx_mm, b + 2)
                        if w is None or w >= 0:
                            wait(act, s_grep[p], 16 * (i + 1))
                        act.activation(g_stage[:, NIP:NIP + TOK], pa[0:T, 0:TOK], ACT.Copy)
                        act.activation(g_stage[:, 0:NIP], pa[0:T, T:TOK], ACT.Copy).then_inc(s_gstage, 1)
                        wait(act, s_vcopy, b + 1)
                        act.activation(v_stage[:, :], pa[0:T, TOK:TOK + C], ACT.Copy)
                        act.activation(k_split[0:T, :, :, 0, :], doubled(pa[0:T, TOK + C:TOK + 2 * C]),
                                       ACT.Copy).then_inc(s_khi, 1)
                    if g == 3 and has(w) and has(w, ahead=1):
                        wait(act, s_qT, b + 2)
                        act.activation(q_stack[n][:, 0:G - 1, :].rearrange("r g t -> r (g t)"), pa[:, :],
                                       ACT.Copy).then_inc(s_qst03, 1)
                    if g == 4 and has(w) and has(w, ahead=1):
                        wait(act, s_kq4, b + 2)
                        act.activation(k_stack[:, G - 1, :], pb[:, 0:TOK], ACT.Copy)
                        act.activation(q_stack[n][:, G - 1, :], pb[:, TOK:TOK + S], ACT.Copy).then_inc(s_st4, 1)
                    if has_group(w, g, 2):
                        t = grp - 2
                        tp = (p * G + g) % 2
                        wait(act, s_transp, t + 1)
                        wait(act, s_main, PG * t - PG)
                        act.activation(probsT[tp][:, :, :].rearrange("t h s -> t (h s)"), probsT_ps[tp][0:T, :],
                                       ACT.Copy).then_inc(s_probsT, 1)
                    if g == 1 and has(w, ahead=1):
                        wait(act, s_kT, b + 2)
                        if w is None or w >= 0:
                            wait(act, s_kd03[p], 64 * (i + 1))
                            wait(act, s_kd4[p], 64 * (i + 1))
                        if w == -1:
                            wait(act, s_zeros[0], 1)
                            for j in range(HG):
                                rows = slice(32 * j, 32 * j + 32)
                                last = act.activation(k_diag[0][rows, 0:G - 1, j, :],
                                                      pa[rows, :].rearrange("r (g t) -> r g t", t=TOK), ACT.Copy)
                                if j < HG - 1:
                                    last.then_inc(s_kd03[0], 32 if j == 0 else 16)
                            last.then_inc(s_kst03, 1)
                        else:
                            act.activation(k_stack[:, 0:G - 1, :].rearrange("r g t -> r (g t)"), pa[:, :],
                                           ACT.Copy).then_inc(s_kst03, 1)
                    if g == 2 and has(w, lag=2):
                        wait(act, s_centred, b - 1)
                        wait(act, s_ipprobs, 2 * (b - 2))
                        act.activation(ip_exp[:, :, :], centred[:, :, :], ACT.Exp).then_inc(s_ipexp, 1)
                    if has(w):
                        act.wait_ge(s_max, grp + 1)
                        for j in range(HG):
                            h = HG * g + j
                            last = act.activation(probs[p][:, h, :], score_ps[(p * G + g) % 2][:, j * TOK:j * TOK + T],
                                                  ACT.Exp, bias=negmax[p][:, h:h + 1])
                        last.then_inc(s_exp, 1)
                    if g == 0 and has(w, ahead=1):
                        wait(act, s_q_mm, b + 2)
                        act.activation(q_split[:, :, 0, :, :], doubled(pb[:, 0:C]),
                                       ACT.Copy).then_inc(s_qhi, 1)

            windows(act, window)

        @block.vector
        def _(dve):
            dve.memset(k_diag[0][:, :, :, :].bitcast(F32), 0.0).then_inc(s_zeros[0], 1)
            dve.wait_ge(s_ipn_in, 16)
            dve.tensor_tensor_reduce(ip_junk[:, :], ip_sb[:, :], ip_sb[:, :], 1.0, 0.0, ALU.mult, ALU.add,
                                     ip_ss[:, 0:1]).then_inc(s_ipnorm, 1)
            dve.wait_ge(s_ipnorm, 1)
            dve.tensor_scalar(ip_ss[:, 1:2], ip_ss[:, 0:1], EPS2, None, ALU.max).then_inc(s_ipnorm, 1)
            dve.wait_ge(s_iprn, 1)
            dve.tensor_scalar(ipunit[:, :], ip_sb[:, :], ip_ss[:, 2:3], 0.5, ALU.mult, ALU.mult).then_inc(s_ipunit, 1)
            dve.wait_ge(s_ipunit_T, 1)
            dve.tensor_copy(ipunitT[:, :, :].rearrange("p c t -> p (c t)"),
                            main_ps[1][:, 0:EC * B * NIP]).then_inc(s_ipunitT, 1)
            dve.wait_ge(s_ipk_mm, 1)
            kips = doubled(main_ps[0][0:B * NIP, 0:C])
            dve.tensor_copy(kip_split[:, :, :, 0, :].bitcast(F32R), kips).then_inc(s_kip, 1)
            dve.wait_ge(s_kip, 1)
            dve.tensor_tensor(kip_split[:, :, :, 1, :].bitcast(F32R), kips, kip_split[:, :, :, 0, :],
                              ALU.subtract).then_inc(s_kip, 1)
            dve.wait_ge(s_ipv_mm, 1)
            dve.tensor_copy(vip_sb[:, :], score_ps[0][0:B * NIP, 0:C]).then_inc(s_vip, 1)
            dve.wait_ge(s_ident_in, 16)
            dve.tensor_copy(ident_r_sb[:, :], ident_sb[:, :])
            dve.wait_ge(s_fill, 3)
            dve.wait_ge(s_wq_in, 16)
            dve.tensor_scalar(wq_scaled[:, :, :], wq_sb[:, :, :], SCALE, None, ALU.mult).then_inc(s_wq, 1)

            def stats(b, n, g0, g1, before):
                heads = slice(HG * g0, HG * g1)

                def paired(t):
                    return t[:, heads].rearrange("s (r a) -> s r a", a=2)

                den = bass.AP(small[n], NIP + PG * g0 * SMALL, [[NPAIR * SMALL, S], [SMALL, PG * (g1 - g0)], [2 * D + 1, 2]])
                wait(dve, s_norm, NPAIR * (b - 1) + PG * g1)
                wait(dve, s_text, b - 1)
                wait(dve, s_rnorm, b - 1)
                dve.scalar_tensor_tensor(out=paired(guard), in0=den, scalar=EPS2, in1=den, op0=ALU.mult,
                                         op1=ALU.mult).then_inc(s_stats, 1)
                dve.reciprocal(paired(rden), den).then_inc(s_stats, 1)
                wait(dve, s_stats, before + 1)
                dve.tensor_tensor(clamped[:, heads], norm2[n][:, heads], guard[:, heads], ALU.max).then_inc(s_stats, 1)

            def window(b, p, i, w):
                n = 1 - p
                for g in range(G):
                    grp = b * G + g
                    if g == 2 and has(w, ahead=1):
                        wait(dve, s_qhi, b + 2)
                        dve.tensor_tensor(q_split[:, :, 1, :, :], doubled(pb[:, 0:C]),
                                          q_split[:, :, 0, :, :], ALU.subtract).then_inc(s_qlo, 1)
                    if g == 2 and w == B:
                        stats(b, n, 0, PARTED, 3 * (b - 1))
                    if g == (3 if w is None or w <= B else 0) and has(w, lag=3):
                        if w is not None and w >= B:
                            ip_output(dve, b, p, i)
                        wait(dve, s_ipout, 3 * (b - 2))
                        wait(dve, s_text, b - 2)
                        wait(dve, s_oT_tr, b - 3)
                        dve.tensor_tensor(attn_out[:, :], ip_out[:, :], text[n][:, :], ALU.add).then_inc(s_attn, 1)
                    if g == 4 and has(w, lag=2):
                        wait(dve, s_ipsum, 2 * (b - 1))
                        wait(dve, s_ipprobs, 2 * (b - 2))
                        dve.reciprocal(rip[:, :], ipsum[:, :]).then_inc(s_rip, 1)
                    if g == 4 and has(w, lag=1):
                        if w == B:
                            stats(b, n, PARTED, G, 3 * b)
                        else:
                            stats(b, n, 0, G, 3 * (b - 1))
                    if g == 4 and has(w, lag=3):
                        wait(dve, s_final_mm, b - 2)
                        wait(dve, s_xn_in[n], 16 * (i - 1 + p))
                        wait(dve, s_store[n], 16 * (i - 2 + p))
                        dve.tensor_tensor(out_sb[n][:, :], pb[:, 0:C], xn_sb[n][:, :], ALU.add).then_inc(s_final, 1)
                    if has_group(w, g, 4):
                        wb = p if g >= 4 else n
                        gg = (g - 4) % G
                        if gg == 0:
                            wait(dve, s_text, b - 1)
                        for r in range(PG):
                            pair = grp * PG + r - 4 * PG
                            wait(dve, s_norm, pair - 1)
                            wait(dve, s_main, pair + 1)
                            for a in range(2):
                                h = HG * gg + 2 * r + a
                                u = main_ps[r][:, a * (T + SMALL):a * (T + SMALL) + T]
                                dve.tensor_tensor_reduce(junk[:, 2 * r + a, :], u, probs[wb][:, h, :], 1.0, 0.0, ALU.mult,
                                                         ALU.add, norm2[wb][:, h:h + 1])
                            dve.tensor_copy(small[wb][:, PG * gg + r, :],
                                            main_ps[r][:, T:T + SMALL]).then_inc(s_norm, 1)
                    if g == 1 and has(w, lag=2):
                        wait(dve, s_fuse, 2 * (b - 1))
                        dve.tensor_reduce(ipmax[:, :], fused[:, :, :], AX_X, ALU.max).then_inc(s_ipmax, 1)
                    if g == 3 and has(w, lag=3):
                        wait(dve, s_oT_tr, b - 2)
                        wait(dve, s_final_mm, b - 3)
                        dve.tensor_copy(oT[0:CH, :, :].rearrange("c a s -> c (a s)"), pb[0:CH, 0:2 * S]).then_inc(s_oT, 1)
                    if has(w):
                        wait(dve, s_scores, grp + 1)
                        if g == 0:
                            wait(dve, s_ipstage, b - 1)
                        sc = score_ps[(p * G + g) % 2][:, :].rearrange("s (h t) -> s h t", t=TOK)
                        dve.tensor_copy(ip_score[p][:, HG * g:HG * g + HG, :], sc[:, :, T:TOK])
                        dve.tensor_reduce(negmax[p][:, HG * g:HG * g + HG], sc[:, :, 0:T], AX_X, ALU.max,
                                          negate=True).then_inc(s_max, 1)
                    if g == 0 and has(w, ahead=1):
                        wait(dve, s_khi, b + 2)
                        dve.tensor_tensor(k_split[0:T, :, :, 1, :], doubled(pa[0:T, TOK + C:TOK + 2 * C]),
                                          k_split[0:T, :, :, 0, :], ALU.subtract).then_inc(s_klo, 1)
                    if g == 3 and w == -1:
                        wait(dve, s_kq4, 1)
                        for j in range(HG):
                            rows = slice(32 * j, 32 * j + 32)
                            dve.tensor_copy(k_diag[0][rows, G - 1, j, :], pb[rows, 0:TOK]).then_inc(s_kd4[0], 16)
                        dve.tensor_copy(q_stack[0][:, G - 1, :], pb[:, TOK:TOK + S]).then_inc(s_st4, 1)
                        wait(dve, s_qT, 1)
                        dve.tensor_copy(q_stack[0][:, 0:G - 1, :].rearrange("r g t -> r (g t)"),
                                        main_ps[1][:, :]).then_inc(s_qst03, 1)

            windows(dve, window)

        @block.tensor
        def _(pe):
            pe.wait_ge(s_ipw_in, 16 * 2)
            for c in range(EC):
                mm = pe.matmul(main_ps[0][0:B * NIP, 0:C], ipT_sb[:, c, :], wkvip_sb[:, c, 0:C],
                               start=(c == 0), stop=(c == EC - 1))
            mm.then_inc(s_ipk_mm, 1)
            pe.wait_ge(s_ident_in, 16)
            pe.wait_ge(s_ipunit, 1)
            for c in range(EC):
                mm = pe.transpose(main_ps[1][:, c * B * NIP:(c + 1) * B * NIP], ipunit[:, c * 128:(c + 1) * 128],
                                  ident_sb[0:B * NIP, 0:B * NIP])
            mm.then_inc(s_ipunit_T, 1)
            for c in range(EC):
                mm = pe.matmul(score_ps[0][0:B * NIP, 0:C], ipT_sb[:, c, :], wkvip_sb[:, c, C:2 * C],
                               start=(c == 0), stop=(c == EC - 1))
            mm.then_inc(s_ipv_mm, 1)
            pe.wait_ge(s_wkv_in, 16)

            def stacked(split, g):
                return split[:, HG * g:HG * g + HG, :, :, :].rearrange("t h a b d -> t (h a b d)")

            def window(b, p, i, w):
                n = 1 - p
                for g in range(G):
                    grp = b * G + g
                    if g == 0 and has(w, ahead=1):
                        wait(pe, s_ctx_in[n], 16 * (i + p + 1))
                        wait(pe, s_ipcol, b + 2)
                        if w == 0:
                            wait(pe, s_kst03, 1)
                        wait(pe, s_qst03, b + 1)
                        for lo, width, rhs in ((0, TOK, None), (TOK, C, 0), (TOK + C, C, C)):
                            for c in range(EC):
                                r = ctxT_sb[n][:, c, :] if rhs is None else wkv_sb[:, c, rhs:rhs + C]
                                mm = pe.matmul(pa[:, lo:lo + width], ctxT_sb[n][:, c, :], r, start=(c == 0), stop=(c == EC - 1))
                        mm.then_inc(s_ctx_mm, 1)
                    if g == 3 and has(w, lag=3):
                        wait(pe, s_attn, b - 2)
                        if has(w, ahead=1):
                            wait(pe, s_qlo, b + 2)
                        wait(pe, s_final, b - 3)
                        for c in range(2):
                            mm = pe.transpose(pb[0:CH, c * S:(c + 1) * S], attn_out[:, c * CH:(c + 1) * CH], ident_sb[:, :])
                        mm.then_inc(s_oT_tr, 1)
                    if has(w):
                        if w == 0 and g == 0:
                            wait(pe, s_kst03, 1)
                        if g == 0:
                            wait(pe, s_kd03[p], 64 * (i + 1))
                            wait(pe, s_qst03, b + 1)
                        if g == G - 1:
                            wait(pe, s_kd4[p], 64 * (i + 1))
                        wait(pe, s_exp, grp - 1)
                        pe.matmul(score_ps[(p * G + g) % 2][:, :], q_stack[p][:, g, :],
                                  k_diag[p][:, g, :, :].rearrange("r h t -> r (h t)"), start=True,
                                  stop=True).then_inc(s_scores, 1)
                    if g == 4 and has(w, ahead=1):
                        wait(pe, s_final, b - 2)
                        wait(pe, s_qlo, b + 2)
                        pe.matmul(pb[:, 0:TOK], stacked(k_split, G - 1), ident_r_sb[:, :], start=True, stop=True)
                        pe.matmul(pb[:, TOK:TOK + S], stacked(q_split, G - 1), ident_r_sb[:, :], start=True,
                                  stop=True).then_inc(s_kq4, 1)
                    if has_group(w, g, 2):
                        tg, tb = (g - 2) % G, (p if g >= 2 else n)
                        tp = (p * G + g) % 2
                        wait(pe, s_exp, grp - 1)
                        wait(pe, s_probsT, grp - 3)
                        for j in range(HG):
                            mm = pe.transpose(probsT_ps[tp][0:T, j * S:(j + 1) * S], probs[tb][:, HG * tg + j, :],
                                              ident_sb[:, :])
                        mm.then_inc(s_transp, 1)
                    if g == 3 and has(w, lag=3):
                        if w == 3:
                            pe.wait_ge(s_const_in, 16 * 2)
                        wait(pe, s_oT, b - 2)
                        for c in range(2):
                            mm = pe.matmul(pb[:, 0:C], oT[:, c, :], wout_sb[:, c, :], start=(c == 0), stop=(c == 1))
                        mm.then_inc(s_final_mm, 1)
                    if has_group(w, g, 3):
                        mg, mb = (g - 3) % G, (p if g >= 3 else n)
                        mp = (p * G + g - 3) % 2
                        if mg == 0:
                            wait(pe, s_grep[mb], 16 * (i + 1))
                            wait(pe, s_vcopy, b + 1)
                        wait(pe, s_probsT, grp - 2)
                        for r in range(PG):
                            pair = grp * PG + r - 3 * PG
                            wait(pe, s_norm, pair - 1)
                            blk = main_rhs[mb][:, PG * mg + r, :]
                            pe.matmul(main_ps[r][:, 0:MAIN], probsT[mp][:, 2 * r, :], blk[:, RW - MAIN:RW],
                                      start=True, stop=True)
                            pe.matmul(main_ps[r][:, MAIN:2 * MAIN], probsT[mp][:, 2 * r + 1, :], blk[:, 0:MAIN],
                                      start=True, stop=True).then_inc(s_main, 1)
                    if g == 0 and has(w, ahead=1):
                        if w == -1:
                            wait(pe, s_wq, 1)
                        wait(pe, s_xT_in[n], 16 * (i + p + 1))
                        wait(pe, s_final, b - 3)
                        wait(pe, s_st4, b + 1)
                        for c in range(2):
                            mm = pe.matmul(pb[:, 0:C], xT_sb[n][:, c, :], wq_scaled[:, c, :], start=(c == 0), stop=(c == 1))
                        mm.then_inc(s_q_mm, 1)
                    if g == 1 and has(w, ahead=1):
                        wait(pe, s_klo, b + 2)
                        wait(pe, s_kip_in, 16 * (b + 2))
                        for k in range(G - 1):
                            mm = pe.matmul(pa[:, k * TOK:(k + 1) * TOK], stacked(k_split, k), ident_r_sb[:, :],
                                           start=True, stop=True)
                        mm.then_inc(s_kT, 1)
                    if g == 2 and has(w, ahead=1):
                        wait(pe, s_qlo, b + 2)
                        if w != -1:
                            wait(pe, s_kst03, b + 2)
                        bank_q = main_ps[1] if w == -1 else pa
                        for k in range(G - 1):
                            mm = pe.matmul(bank_q[:, k * S:(k + 1) * S], stacked(q_split, k), ident_r_sb[:, :],
                                           start=True, stop=True)
                        mm.then_inc(s_qT, 1)

            windows(pe, window)


def kernel(x, ctx_2048, fside_S_0, L0_xattn_W_q, L0_xattn_W_k, L0_xattn_W_v, L0_xattn_W_k_ip, L0_xattn_W_v_ip,
           L0_xattn_W_out, L0_xattn_b_out):
    import numpy as np
    import concourse.bacc as bacc
    from concourse.bass_utils import run_bass_kernel_spmd

    def chunks(a, n):
        return np.ascontiguousarray(np.moveaxis(a.reshape(n, a.shape[0] // n, *a.shape[1:]), 0, 1))

    x = np.asarray(x)
    cx = np.asarray(ctx_2048)
    wk, wv, wkip, wvip = (np.asarray(a) for a in (L0_xattn_W_k, L0_xattn_W_v, L0_xattn_W_k_ip, L0_xattn_W_v_ip))
    wv_swapped = wv.reshape(E, NPAIR, 2, D)[:, :, ::-1].reshape(E, C)
    wout = np.asarray(L0_xattn_W_out)
    wout_rows = np.zeros((CH + 1, 2, C), np.float32)
    wout_rows[:CH] = chunks(wout, 2)
    wout_rows[CH, 1] = np.asarray(L0_xattn_b_out)
    ip = np.ascontiguousarray(cx[:, T:].reshape(B * NIP, E))
    arrays = {
        "xT": np.ascontiguousarray(x.reshape(B, S, 2, CH).transpose(0, 3, 2, 1)),
        "xn": np.ascontiguousarray(x),
        "ctxT": np.ascontiguousarray(cx[:, :T].reshape(B, T, EC, 128).transpose(0, 3, 2, 1)),
        "ipT": np.ascontiguousarray(ip.reshape(B * NIP, EC, 128).transpose(2, 1, 0)),
        "ipn": ip,
        "smask": np.ascontiguousarray(np.asarray(fside_S_0).reshape(S, 1)),
        "wq": chunks(np.asarray(L0_xattn_W_q), 2),
        "wkv": chunks(np.concatenate([wv_swapped, wk], 1), EC),
        "wkvip": chunks(np.concatenate([wkip, wvip], 1), EC),
        "wout": wout_rows,
        "ident": np.eye(128, dtype=np.float32),
    }
    nc = bacc.Bacc("TRN2", target_bir_lowering=False, num_devices=1)
    args = {name: nc.dram_tensor(name, a.shape, mybir.dt.from_np(a.dtype), kind="ExternalInput").ap()
            for name, a in arrays.items()}
    kip_d = nc.dram_tensor("kip_d", (B * NIP, 4 * C), F32, kind="Internal").ap()
    vip_d = nc.dram_tensor("vip_d", (B * NIP, C), F32, kind="Internal").ap()
    out = nc.dram_tensor("out", (B, S, C), F32, kind="ExternalOutput").ap()
    xattn_program(nc, **args, kip_d=kip_d, vip_d=vip_d, out=out)
    r = run_bass_kernel_spmd(nc, [arrays], core_ids=[0])
    return r.results[0]["out"]
```
